# Optimizing a Trainium2 kernel written in Bass

```python
import numpy as np
import jax
import jax.numpy as jnp

def _softmax(x, axis=-1):
    return jax.nn.softmax(x, axis=axis)
def _gelu(x):
    return jax.nn.gelu(x, approximate=True)
def _silu(x):
    return jax.nn.silu(x)
def _sigmoid(x):
    return jax.nn.sigmoid(x)
def _layernorm(x, axis=-1, eps=1e-5):
    m = jnp.mean(x, axis=axis, keepdims=True)
    v = jnp.var(x, axis=axis, keepdims=True)
    return (x - m) / jnp.sqrt(v + eps)
def _scatter_add(tgt, idx, src, axis=0):
    return tgt.at[idx].add(src)
def _segment_sum(src, seg, n):
    return jax.ops.segment_sum(src, seg, n)

kernel_name = 'mk_conv_seq_d2_conv_nchw512_6e242d'

def setup_inputs(seed: int = 0):
    np.random.seed(seed)
    _w = jnp.asarray
    def _rec_inputs():
        import jax
        import jax.numpy as jnp
        _gk = jax.random.key(seed)
        x = -0.0006537 + 1.001 * jax.random.normal(jax.random.fold_in(_gk, 1), (2, 512, 48, 48), jnp.float32)
        return x
    x = _rec_inputs()
    def _L0_conv_setup():
        import jax, jax.numpy as jnp
        import numpy as np
        B, C, H, W = (2, 512, 48, 48)
        HEADS = 8
        GROUPS = 32
        EPS = 1e-05

        def _group_norm(x, w, b):
            b_, c_, h_, w_ = x.shape
            xg = x.reshape(b_, GROUPS, c_ // GROUPS, h_, w_)
            mean = xg.mean(axis=(2, 3, 4), keepdims=True)
            var = xg.var(axis=(2, 3, 4), keepdims=True)
            xn = ((xg - mean) * jax.lax.rsqrt(var + EPS)).reshape(b_, c_, h_, w_)
            return xn * w[None, :, None, None] + b[None, :, None, None]
        key = jax.random.key(seed)
        ks = jax.random.split(key, 5)
        return {'x': jax.random.normal(ks[0], (B, C, H, W), jnp.float32), 'gn_w': jnp.ones((C,), jnp.float32), 'gn_b': jnp.zeros((C,), jnp.float32), 'qkv_w': jax.random.normal(ks[1], (3 * C, C), jnp.float32) / np.float32(np.sqrt(C)), 'qkv_b': jax.random.normal(ks[2], (3 * C,), jnp.float32) * 0.01, 'proj_w': jax.random.normal(ks[3], (C, C), jnp.float32) / np.float32(np.sqrt(C)), 'proj_b': jax.random.normal(ks[4], (C,), jnp.float32) * 0.01}
    _L0_conv_all = _L0_conv_setup()
    _L0_conv_in = {k: v for k, v in _L0_conv_all.items() if k in ('gn_w', 'gn_b', 'qkv_w', 'qkv_b', 'proj_w', 'proj_b', )}
    del _L0_conv_all

    def _L1_conv_setup():
        import jax, jax.numpy as jnp
        import numpy as np
        FREQ_DIM = 32
        TIME_DIM = 32
        HEADS = 8
        TWO_PI = 6.283185307179586

        def get_embeddings(B, H, W, freq_dim, time_dim, dtype):
            nf = freq_dim // 2
            ln_x = jnp.log2(jnp.arange(0, H * nf, dtype=jnp.float32))
            ln_x = ln_x.at[0].set(-2.0)
            ln_x = ln_x.reshape(H, nf).T
            ln_x = ln_x * jnp.arange(1, nf + 1, dtype=jnp.float32)[:, None]
            freq = jnp.stack([jnp.cos(ln_x), jnp.sin(ln_x)], axis=1).reshape(freq_dim, H)
            freq = jnp.broadcast_to(freq[None, :, :, None], (B, freq_dim, H, W))
            nt = time_dim // 2
            k = jnp.arange(0, nt, dtype=jnp.float32) + 0.5
            x = jnp.arange(0, nt * W, dtype=jnp.float32).reshape(W, nt).T
            theta = k[:, None] * x / (W * nt) * TWO_PI
            time = jnp.stack([jnp.cos(theta), jnp.sin(theta)], axis=1).reshape(time_dim, W)
            time = jnp.broadcast_to(time[None, :, None, :], (B, time_dim, H, W))
            return jnp.concatenate([freq, time], axis=1).astype(dtype)
        key = jax.random.key(seed)
        ks = jax.random.split(key, 6)
        B, C, H, W = (2, 512, 64, 32)
        qkC = C + FREQ_DIM + TIME_DIM
        inner = HEADS * 64
        return {'hidden_states': jax.random.normal(ks[0], (B, C, H, W), dtype=jnp.float32), 'Wq': jax.random.normal(ks[1], (qkC, inner), dtype=jnp.float32) * 0.02, 'Wk': jax.random.normal(ks[2], (qkC, inner), dtype=jnp.float32) * 0.02, 'Wv': jax.random.normal(ks[3], (C, inner), dtype=jnp.float32) * 0.02, 'Wout': jax.random.normal(ks[4], (inner, C), dtype=jnp.float32) * 0.02, 'bout': jnp.zeros((C,), dtype=jnp.float32)}
    _L1_conv_all = _L1_conv_setup()
    _L1_conv_in = {k: v for k, v in _L1_conv_all.items() if k in ('Wq', 'Wk', 'Wv', 'Wout', 'bout', )}
    del _L1_conv_all

    return {
        "x": x,
        "L0_conv_gn_w": _L0_conv_in["gn_w"],
        "L0_conv_gn_b": _L0_conv_in["gn_b"],
        "L0_conv_qkv_w": _L0_conv_in["qkv_w"],
        "L0_conv_qkv_b": _L0_conv_in["qkv_b"],
        "L0_conv_proj_w": _L0_conv_in["proj_w"],
        "L0_conv_proj_b": _L0_conv_in["proj_b"],
        "L1_conv_Wq": _L1_conv_in["Wq"],
        "L1_conv_Wk": _L1_conv_in["Wk"],
        "L1_conv_Wv": _L1_conv_in["Wv"],
        "L1_conv_Wout": _L1_conv_in["Wout"],
        "L1_conv_bout": _L1_conv_in["bout"],
    }

def reference(x, L0_conv_gn_w, L0_conv_gn_b, L0_conv_qkv_w, L0_conv_qkv_b, L0_conv_proj_w, L0_conv_proj_b, L1_conv_Wq, L1_conv_Wk, L1_conv_Wv, L1_conv_Wout, L1_conv_bout):
    import jax
    import jax.numpy as jnp
    def _L0_conv_ref(x, gn_w, gn_b, qkv_w, qkv_b, proj_w, proj_b):
        import jax, jax.numpy as jnp
        import numpy as np
        B, C, H, W = (2, 512, 48, 48)
        HEADS = 8
        GROUPS = 32
        EPS = 1e-05

        def _group_norm(x, w, b):
            b_, c_, h_, w_ = x.shape
            xg = x.reshape(b_, GROUPS, c_ // GROUPS, h_, w_)
            mean = xg.mean(axis=(2, 3, 4), keepdims=True)
            var = xg.var(axis=(2, 3, 4), keepdims=True)
            xn = ((xg - mean) * jax.lax.rsqrt(var + EPS)).reshape(b_, c_, h_, w_)
            return xn * w[None, :, None, None] + b[None, :, None, None]
        bx, cx, hx, wx = x.shape
        d = cx // HEADS
        n = hx * wx
        xn = _group_norm(x, gn_w, gn_b)
        y = jnp.einsum('oc,bchw->bohw', qkv_w, xn) + qkv_b[None, :, None, None]
        qkv = y.reshape(bx * HEADS, d, 3, n)
        q, k, v = (qkv[:, :, 0, :], qkv[:, :, 1, :], qkv[:, :, 2, :])
        scale = np.float32(1.0 / np.sqrt(d))
        w_attn = jax.nn.softmax(jnp.einsum('ncq,nck->nqk', q, k * scale), axis=2)
        a = jnp.einsum('nqk,nck->ncq', w_attn, v).reshape(bx, cx, hx, wx)
        out = jnp.einsum('oc,bchw->bohw', proj_w, a) + proj_b[None, :, None, None]
        return out + x

    def _L1_conv_ref(hidden_states, Wq, Wk, Wv, Wout, bout):
        import jax, jax.numpy as jnp
        import numpy as np
        FREQ_DIM = 32
        TIME_DIM = 32
        HEADS = 8
        TWO_PI = 6.283185307179586

        def get_embeddings(B, H, W, freq_dim, time_dim, dtype):
            nf = freq_dim // 2
            ln_x = jnp.log2(jnp.arange(0, H * nf, dtype=jnp.float32))
            ln_x = ln_x.at[0].set(-2.0)
            ln_x = ln_x.reshape(H, nf).T
            ln_x = ln_x * jnp.arange(1, nf + 1, dtype=jnp.float32)[:, None]
            freq = jnp.stack([jnp.cos(ln_x), jnp.sin(ln_x)], axis=1).reshape(freq_dim, H)
            freq = jnp.broadcast_to(freq[None, :, :, None], (B, freq_dim, H, W))
            nt = time_dim // 2
            k = jnp.arange(0, nt, dtype=jnp.float32) + 0.5
            x = jnp.arange(0, nt * W, dtype=jnp.float32).reshape(W, nt).T
            theta = k[:, None] * x / (W * nt) * TWO_PI
            time = jnp.stack([jnp.cos(theta), jnp.sin(theta)], axis=1).reshape(time_dim, W)
            time = jnp.broadcast_to(time[None, :, None, :], (B, time_dim, H, W))
            return jnp.concatenate([freq, time], axis=1).astype(dtype)
        B, C, H, W = hidden_states.shape
        emb = get_embeddings(B, H, W, FREQ_DIM, TIME_DIM, hidden_states.dtype)
        qk_hs = jnp.concatenate([hidden_states, emb], axis=1)
        S = H * W
        qk_hs = qk_hs.reshape(B, -1, S).transpose(0, 2, 1)
        v_hs = hidden_states.reshape(B, C, S).transpose(0, 2, 1)
        q = qk_hs @ Wq
        k = qk_hs @ Wk
        v = v_hs @ Wv
        hd_qk = q.shape[-1] // HEADS
        hd_v = v.shape[-1] // HEADS
        q = q.reshape(B, S, HEADS, hd_qk).transpose(0, 2, 1, 3)
        k = k.reshape(B, S, HEADS, hd_qk).transpose(0, 2, 1, 3)
        v = v.reshape(B, S, HEADS, hd_v).transpose(0, 2, 1, 3)
        scale = 1.0 / jnp.sqrt(jnp.asarray(hd_qk, dtype=q.dtype))
        scores = jnp.einsum('bhqd,bhkd->bhqk', q, k) * scale
        attn = jax.nn.softmax(scores, axis=-1)
        o = jnp.einsum('bhqk,bhkd->bhqd', attn, v)
        o = o.transpose(0, 2, 1, 3).reshape(B, S, HEADS * hd_v)
        o = o @ Wout + bout
        o = o.transpose(0, 2, 1).reshape(B, C, H, W)
        return o + hidden_states

    def _gn(v, G=32, eps=1e-5):
        B_, C_, H_, W_ = v.shape
        g = v.reshape(B_, G, C_ // G, H_, W_)
        m = jnp.mean(g, axis=(2, 3, 4), keepdims=True)
        s = jnp.var(g, axis=(2, 3, 4), keepdims=True)
        return ((g - m) / jnp.sqrt(s + eps)).reshape(v.shape)

    def _ln_c(v, eps=1e-6):
        m = jnp.mean(v, axis=1, keepdims=True)
        s = jnp.var(v, axis=1, keepdims=True)
        return (v - m) / jnp.sqrt(s + eps)

    def _ln_t(v, eps=1e-5):
        m = jnp.mean(v, axis=-1, keepdims=True)
        s = jnp.var(v, axis=-1, keepdims=True)
        return (v - m) / jnp.sqrt(s + eps)

    def _to_tokens(v):
        B_, C_, H_, W_ = v.shape
        return v.reshape(B_, C_, H_ * W_).transpose(0, 2, 1)
    def _from_tokens(t, like):
        B_, C_, H_, W_ = like.shape
        return t.transpose(0, 2, 1).reshape(B_, C_, H_, W_)

    x = _L0_conv_ref(x, L0_conv_gn_w, L0_conv_gn_b, L0_conv_qkv_w, L0_conv_qkv_b, L0_conv_proj_w, L0_conv_proj_b)
    x = _L1_conv_ref(x, L1_conv_Wq, L1_conv_Wk, L1_conv_Wv, L1_conv_Wout, L1_conv_bout)
    return x


_drawn_inputs = setup_inputs


def setup_inputs(seed=0):
    import zlib

    import numpy as np

    out = dict(_drawn_inputs(seed))
    spreads = {'L0_conv_gn_w': (1.0, 0.6), 'L0_conv_gn_b': (0.0, 0.1), 'L1_conv_bout': (0.0, 0.1)}
    factors = {'L0_conv_qkv_b': 5.713, 'L0_conv_proj_b': 5.627, 'L1_conv_Wq': 8.0, 'L1_conv_Wk': 8.0}
    for name, (base, spread) in spreads.items():
        noise = np.random.default_rng([zlib.crc32(name.encode()), seed]).standard_normal(out[name].shape)
        drawn = base * np.exp(spread * noise) if base else spread * noise
        out[name] = jnp.asarray(drawn.astype(out[name].dtype))
    for name, factor in factors.items():
        out[name] = (out[name] * factor).astype(out[name].dtype)
    return out
```

```python
from contextlib import ExitStack

import concourse.bass as bass
from concourse import mybir

F32 = mybir.dt.float32
F32R = mybir.dt.float32r
ALU = mybir.AluOpType
ACT = mybir.ActivationFunctionType
AX = mybir.AxisListType

P = 128
B, C, HW = 2, 512, 48 * 48
T = B * HW
CT = C // P
D = 64
PAIRS = C // (2 * D)
GROUP = C // 32
CH = 384
NCH = T // CH
TT = CH // P
KT = HW // P
JB = HW // CH
KC = KT // 3
SLOTS = 2 * KC
NB = B * PAIRS * JB
SCALE = float(D) ** -0.5
GN_EPS = 1e-5
SHIFT_DVE = 208
EXP_LAG = 8
PV_LAG = SLOTS + 5

PV_COUNTS = [2, 2, 2, 2, 1, 2, 1, 1, 2, 1, 1, 1]
PV_TILES = [list(range(sum(PV_COUNTS[:v]), sum(PV_COUNTS[:v + 1]))) for v in range(SLOTS)]
DEN_AT = SLOTS - KT // 2
LAST_USE = [max(max(v for v in range(SLOTS) if set(PV_TILES[v]) & {3 * c, 3 * c + 1, 3 * c + 2}),
                DEN_AT + (3 * c + 2) // 2) for c in range(KC)]


INVERT_AT = [0, 1, 2, 4, 5, 6]
PARTS = len(INVERT_AT)


def is_block(t, *numbers):
    return isinstance(t, int) and t in numbers


def sb_(ctx, nc, name, shape, dt=F32):
    return ctx.enter_context(nc.sbuf_tensor(name, shape, dt))


def group_norm_stage(nc, x_sb, par, gmat, x_d):
    with ExitStack() as ctx:
        st = sb_(ctx, nc, "gn_stats", [P, B * CT, JB, 6])
        mv = sb_(ctx, nc, "gn_mv", [P, B * CT, 2])
        dif = sb_(ctx, nc, "gn_dif", [P, B * CT])
        vv = sb_(ctx, nc, "gn_var", [P, B * CT])
        sd = sb_(ctx, nc, "gn_sd", [P, B * CT])
        rs = sb_(ctx, nc, "gn_rstd", [P, B * CT])
        tmp = sb_(ctx, nc, "gn_tmp", [P, B * CT])
        aa = sb_(ctx, nc, "gn_scale", [P, B * CT])
        bb = sb_(ctx, nc, "gn_shift", [P, B * CT])
        pm = ctx.enter_context(nc.psum_tensor("gn_mean", [P, 512], F32))
        pv = ctx.enter_context(nc.psum_tensor("gn_pvar", [P, 512], F32))
        x_in = [ctx.enter_context(nc.semaphore(f"x_in{n}")) for n in range(B * CT)]
        stats = ctx.enter_context(nc.semaphore("stats"))
        mean_mm = ctx.enter_context(nc.semaphore("mean_mm"))
        var_mm = ctx.enter_context(nc.semaphore("var_mm"))
        dev_done = ctx.enter_context(nc.semaphore("dev_done"))
        var_done = ctx.enter_context(nc.semaphore("var_done"))
        root_done = ctx.enter_context(nc.semaphore("root_done"))
        step = ctx.enter_context(nc.semaphore("gn_step"))
        block = ctx.enter_context(nc.Block())
        N = B * CT

        @block.sync
        def _(sp):
            for n in range(N):
                b, c = divmod(n, CT)
                sp.dma_start(x_sb[:, c, b * HW:(b + 1) * HW],
                             x_d[c * P:(c + 1) * P, b * HW:(b + 1) * HW]).then_inc(x_in[n], 16)

        @block.tensor
        def _(pe):
            pe.wait_ge(stats, N)
            nc.tensor.matmul(pm[:, 0:N], gmat[:, :], mv[:, :, 0], start=True, stop=True).then_inc(mean_mm, 1)
            pe.wait_ge(dev_done, 1)
            nc.tensor.matmul(pv[:, 0:N], gmat[:, :], vv[:, :], start=True, stop=True).then_inc(var_mm, 1)

        @block.scalar
        def _(act):
            act.wait_ge(var_done, 1)
            nc.scalar.activation(sd[:, :], vv[:, :], ACT.Sqrt).then_inc(root_done, 1)

        @block.vector
        def _(dve):
            done = [0]

            def then(ins):
                done[0] += 1
                ins.then_inc(step, 1)
                return done[0]

            for n in range(N):
                b, c = divmod(n, CT)
                dve.wait_ge(x_in[n], 16)
                for j in range(JB):
                    k = then(nc.vector.bn_stats(st[:, n, j, :], x_sb[:, c, b * HW + j * CH:b * HW + (j + 1) * CH]))
            dve.wait_ge(step, k)
            for n in range(N):
                nc.vector.bn_aggr(mv[:, n, :], st[:, n, :, :]).then_inc(stats, 1)
            dve.wait_ge(stats, N)
            dve.wait_ge(mean_mm, 1)
            k = then(nc.vector.tensor_tensor(dif[:, :], mv[:, :, 0], pm[:, 0:N], ALU.subtract))
            dve.wait_ge(step, k)
            k = then(nc.vector.tensor_tensor(tmp[:, :], dif[:, :], dif[:, :], ALU.mult))
            dve.wait_ge(step, k)
            nc.vector.tensor_tensor(vv[:, :], tmp[:, :], mv[:, :, 1], ALU.add).then_inc(dev_done, 1)
            dve.wait_ge(var_mm, 1)
            nc.vector.tensor_scalar(vv[:, :], pv[:, 0:N], GN_EPS, None, ALU.add).then_inc(var_done, 1)
            dve.wait_ge(root_done, 1)
            k = then(nc.vector.reciprocal(rs[:, :], sd[:, :]))
            dve.wait_ge(step, k)
            k = then(nc.vector.tensor_tensor(tmp[:, :], rs[:, :], rs[:, :], ALU.mult))
            dve.wait_ge(step, k)
            dve.wait_ge(var_done, 1)
            k = then(nc.vector.tensor_tensor(tmp[:, :], tmp[:, :], vv[:, :], ALU.mult))
            dve.wait_ge(step, k)
            k = then(nc.vector.tensor_scalar(tmp[:, :], tmp[:, :], -0.5, 1.5, ALU.mult, ALU.add))
            dve.wait_ge(step, k)
            k = then(nc.vector.tensor_tensor(rs[:, :], rs[:, :], tmp[:, :], ALU.mult))
            dve.wait_ge(step, k)
            for b in range(B):
                s = slice(b * CT, (b + 1) * CT)
                k = then(nc.vector.tensor_tensor(aa[:, s], rs[:, s], par["gn_w"], ALU.mult))
            dve.wait_ge(step, k)
            k = then(nc.vector.tensor_tensor(tmp[:, :], aa[:, :], pm[:, 0:N], ALU.mult))
            dve.wait_ge(step, k)
            for b in range(B):
                s = slice(b * CT, (b + 1) * CT)
                k = then(nc.vector.tensor_tensor(bb[:, s], par["gn_b"], tmp[:, s], ALU.subtract))
            dve.wait_ge(step, k)
            for n in range(N):
                b, c = divmod(n, CT)
                xs = x_sb[:, c, b * HW:(b + 1) * HW]
                nc.vector.tensor_scalar(xs, xs, aa[:, n:n + 1], bb[:, n:n + 1], ALU.mult, ALU.add)


def load_stage(nc, loads):
    with ExitStack() as ctx:
        loaded = ctx.enter_context(nc.semaphore("const_loaded"))
        block = ctx.enter_context(nc.Block())

        @block.sync
        def _(sp):
            for dst, src in loads:
                sp.dma_start(dst, src).then_inc(loaded, 16)
            sp.wait_ge(loaded, 16 * len(loads))


def chunk_stage(nc, name, psum, bufs, src=None, out_proj=None, qkv=None):
    with ExitStack() as ctx:
        def sem(n):
            return ctx.enter_context(nc.semaphore(f"{name}_{n}"))

        xc, att, res, hl, vo = bufs["xc"], bufs["att"], bufs["res"], bufs["hl"], bufs["vo"]
        att_in = [sem(f"att_in{p}") for p in range(2)]
        res_in = [sem(f"res_in{p}") for p in range(2)]
        xc_ready = sem("xc_ready")
        out_mm = sem("out_mm")
        qk_mm = sem("qk_mm")
        v_mm = sem("v_mm")
        high_done = sem("high_done")
        low_done = sem("low_done")
        v_done = sem("v_done")
        q_stored, k_stored = sem("q_stored"), sem("k_stored")
        v_stored = [sem(f"v_stored{p}") for p in range(2)]
        x_stored = [sem(f"x_stored{p}") for p in range(2)]
        block = ctx.enter_context(nc.Block())
        MT = 2 * CT
        XR = CT if out_proj else 1

        def qk_bank(m):
            return psum[:, m % 4, 0:CH]

        def v_bank(p, tt):
            return psum[:, 4 + (TT * p + tt) % 2, 0:C]

        def out_bank(m):
            return psum[:, 6 + m % 2, 0:CH]

        @block.sync
        def _(sp):
            with sp.Fori(0, NCH // 2) as it:
                for p in range(2):
                    i = 2 * it + p
                    tok = bass.ds(i * CH, CH)
                    if out_proj:
                        sp.wait_ge(out_mm, CT * (2 * it))
                        sp.dma_start(att[p][:, :, :], out_proj["att"].rearrange("(c p) t -> p c t", p=P)[:, :, tok])\
                            .then_inc(att_in[p], 16)
                        sp.wait_ge(xc_ready, XR * (2 * it))
                        sp.dma_start(res[p][:, :, :], out_proj["res"].rearrange("(c p) t -> p c t", p=P)[:, :, tok])\
                            .then_inc(res_in[p], 16)
                for p in range(2):
                    i = 2 * it + p
                    tok = bass.ds(i * CH, CH)
                    if out_proj:
                        sp.wait_ge(xc_ready, XR * (i + 1))
                        sp.dma_start(out_proj["dst"].rearrange("(c p) t -> p c t", p=P)[:, :, tok], xc[p][:, :, :])\
                            .then_inc(x_stored[p], 16)
                    if qkv:
                        for half, stored in ((0, q_stored), (1, k_stored)):
                            sp.wait_ge(low_done, MT * i + CT * (half + 1))
                            sp.dma_start(
                                qkv["qk"].rearrange("m w p t -> p (m w) t")[:, half * MT:(half + 1) * MT, tok],
                                hl[half].rearrange("p m w t -> p (m w) t")).then_inc(stored, 16)
                        sp.wait_ge(v_done, TT * (i + 1))
                        sp.dma_start(qkv["v"][bass.ds(i * CH, CH), :].rearrange("(a p) d -> p a d", p=P),
                                     vo[p][:, :, :]).then_inc(v_stored[p], 16)
            for p in range(2):
                if out_proj:
                    sp.wait_ge(x_stored[p], 16 * (NCH // 2))
                if qkv:
                    sp.wait_ge(v_stored[p], 16 * (NCH // 2))
            if qkv:
                sp.wait_ge(q_stored, 16 * NCH)
                sp.wait_ge(k_stored, 16 * NCH)

        @block.tensor
        def _(pe):
            with pe.Fori(0, NCH // 2) as it:
                for p in range(2):
                    i = 2 * it + p
                    if out_proj:
                        pe.wait_ge(att_in[p], 16 * (it + 1))
                        for m in range(CT):
                            if m >= 2:
                                pe.wait_ge(xc_ready, XR * i + m - 1)
                            for c in range(CT):
                                mm = nc.tensor.matmul(out_bank(m), out_proj["w"][:, c, m * P:(m + 1) * P],
                                                      att[p][:, c, :], start=(c == 0), stop=(c == CT - 1))
                            mm.then_inc(out_mm, 1)
                    pe.wait_ge(xc_ready, XR * (i + 1))
                    if not qkv:
                        continue
                    for m in range(MT):
                        if m >= 4:
                            pe.wait_ge(low_done, MT * i + m - 3)
                        elif m == 0:
                            pe.wait_ge(low_done, MT * i)
                        for c in range(CT):
                            mm = nc.tensor.matmul(qk_bank(m), qkv["w"][:, c, m * P:(m + 1) * P], xc[p][:, c, :],
                                                  start=(c == 0), stop=(c == CT - 1 and not qkv["emb"]))
                        if qkv["emb"]:
                            e = qkv["emb"]
                            mm = nc.tensor.matmul(qk_bank(m), e["w"][:, m * P:(m + 1) * P],
                                                  e["x"][:, bass.ds(i * CH, CH)], start=False, stop=True)
                        mm.then_inc(qk_mm, 1)
                    for tt in range(TT):
                        if tt >= 2:
                            pe.wait_ge(v_done, TT * i + tt - 1)
                        elif tt == 0:
                            pe.wait_ge(v_done, TT * i)
                        for c in range(CT):
                            mm = nc.tensor.matmul(v_bank(p, tt), xc[p][:, c, tt * P:(tt + 1) * P], qkv["wv"][:, c, :],
                                                  start=(c == 0), stop=(c == CT - 1))
                        mm.then_inc(v_mm, 1)

        @block.scalar
        def _(act):
            if not qkv:
                return
            with act.Fori(0, NCH // 2) as it:
                for p in range(2):
                    i = 2 * it + p
                    for m in range(MT):
                        half, mm = divmod(m, CT)
                        if mm == 0:
                            act.wait_ge((q_stored, k_stored)[half], 16 * i)
                        act.wait_ge(qk_mm, MT * i + m + 1)
                        high = hl[half][:, mm, 0, :].bitcast(F32R)
                        if qkv["bias"] is not None:
                            a = nc.scalar.activation(high, qk_bank(m), ACT.Identity, bias=qkv["bias"][:, m:m + 1])
                        else:
                            a = nc.scalar.activation(high, qk_bank(m), ACT.Copy)
                        a.then_inc(high_done, 1)

        @block.vector
        def _(dve):
            with dve.Fori(0, NCH // 2) as it:
                for p in range(2):
                    i = 2 * it + p
                    if out_proj:
                        dve.wait_ge(res_in[p], 16 * (it + 1))
                        dve.wait_ge(x_stored[p], 16 * it)
                        if qkv:
                            dve.wait_ge(v_mm, TT * (2 * it))
                        for m in range(CT):
                            dve.wait_ge(out_mm, CT * i + m + 1)
                            nc.vector.scalar_tensor_tensor(
                                out=xc[p][:, m, :], in0=out_bank(m), scalar=out_proj["bias"][:, m:m + 1],
                                in1=res[p][:, m, :], op0=ALU.add, op1=ALU.add).then_inc(xc_ready, 1)
                    else:
                        dve.wait_ge(v_mm, TT * (2 * it))
                        nc.vector.tensor_copy(xc[p][:, :, :], src[:, :, bass.ds(i * CH, CH)]).then_inc(xc_ready, 1)
                    if not qkv:
                        continue
                    for m in range(MT):
                        half, mm = divmod(m, CT)
                        dve.wait_ge(high_done, MT * i + m + 1)
                        high, low = hl[half][:, mm, 0, :], hl[half][:, mm, 1, :].bitcast(F32R)
                        if qkv["bias"] is not None:
                            d = nc.vector.scalar_tensor_tensor(out=low, in0=qk_bank(m), scalar=qkv["bias"][:, m:m + 1],
                                                               in1=high, op0=ALU.add, op1=ALU.subtract)
                        else:
                            d = nc.vector.tensor_tensor(low, qk_bank(m), high, ALU.subtract)
                        d.then_inc(low_done, 1)
                    for tt in range(TT):
                        if tt == 0:
                            dve.wait_ge(v_stored[p], 16 * it)
                        dve.wait_ge(v_mm, TT * i + tt + 1)
                        if qkv["bv"] is not None:
                            d = nc.vector.tensor_tensor(vo[p][:, tt, :], v_bank(p, tt), qkv["bv"][:, :], ALU.add)
                        else:
                            d = nc.vector.tensor_copy(vo[p][:, tt, :], v_bank(p, tt))
                        d.then_inc(v_done, 1)


def attention_stage(nc, name, psum, bufs, qk_d, v_d, att_d):
    with ExitStack() as ctx:
        def sem(n):
            return ctx.enter_context(nc.semaphore(f"{name}_{n}"))

        kst, qst, vst, prob = bufs["kst"], bufs["qst"], bufs["vst"], bufs["prob"]
        run, fold, mx = bufs["run"], bufs["fold"], bufs["mx"]
        den, dsp, pvr, rec, ob = bufs["den"], bufs["dsp"], bufs["pvr"], bufs["rec"], bufs["ob"]
        ones, sel = bufs["ones"], bufs["sel"]
        q_in = [sem(f"q_in{p}") for p in range(2)]
        k_in = [sem(f"k_in{c}") for c in range(KC)]
        v_in = [sem(f"v_in{c}") for c in range(KC)]
        scored = sem("scored")
        copied = sem("copied")
        maxed = sem("maxed")
        folded = sem("folded")
        reducing = sem("reducing")
        mx_ready = sem("mx_ready")
        dve_shifted, pool_shifted = sem("dve_shifted"), sem("pool_shifted")
        exp_done = sem("exp_done")
        pv_done = sem("pv_done")
        den_copied, pv_copied = sem("den_copied"), sem("pv_copied")
        spread = sem("spread")
        spread_copied = sem("spread_copied")
        inverted = sem("inverted")
        normed = sem("normed")
        stored = [sem(f"stored{p}") for p in range(2)]
        block = ctx.enter_context(nc.Block())

        def scored_count(g):
            return SLOTS + g + 1

        def pv_count(t, v):
            return 2 * SLOTS + SLOTS * t + v + 1

        def shifted_count(g):
            return SLOTS + g + 1

        def s_bank(g):
            return psum[:, 3 * (g % 2):3 * (g % 2) + 3, 0:CH]

        pv_bank = psum[:, 6, 0:CH]
        den_bank = psum[:, 7, 0:CH]

        def chunk_of(par, s):
            e, c = divmod(s, KC)
            return prob[par][:, e, 3 * c:3 * c + 3, :]

        def parity(par, s):
            return (par + s // SLOTS) % 2, s % SLOTS

        def shift_part(engine, x, e, q0, q1):
            return engine.tensor_tensor(x[:, :, q0:q1], x[:, :, q0:q1],
                                        mx[e][:, q0:q1].unsqueeze(1).broadcast_to([P, 3, q1 - q0]), ALU.subtract)

        @block.sync
        def _(sp):
            with sp.Fori(0, B) as b, sp.Fori(0, PAIRS) as hp:
                pair = b * PAIRS + hp
                for j in range(JB):
                    t = pair * JB + j
                    sp.wait_ge(scored, scored_count(SLOTS * t - SLOTS - 1))
                    for half in range(2):
                        sp.dma_start(
                            qst[j % 2][half * D:(half + 1) * D, :, :].bitcast(F32),
                            qk_d[bass.ds(hp, 1), :, :, bass.ds(b * HW + j * CH, CH)]
                            .rearrange("m w (e p) t -> p (m w e) t", e=2)).then_inc(q_in[j % 2], 16)
                    if j == 0:
                        for c in range(KC):
                            sp.wait_ge(scored, scored_count(SLOTS * (t - 1) + KC + c))
                            for w in range(2):
                                sp.dma_start(
                                    kst[w * D:(w + 1) * D, :, c * CH:(c + 1) * CH].bitcast(F32),
                                    qk_d[bass.ds(PAIRS + hp, 1), w, :, bass.ds(b * HW + c * CH, CH)]
                                    .rearrange("m (e p) t -> p (m e) t", e=2)).then_inc(k_in[c], 16)
                    if j == 1:
                        for c in range(KC):
                            sp.wait_ge(pv_done, pv_count(t - 2, LAST_USE[c]))
                            sp.dma_start(
                                vst[:, 3 * c:3 * c + 3, :],
                                v_d[bass.ds(b * HW + c * CH, CH), bass.ds(hp * P, P)]
                                .rearrange("(a p) d -> p a d", p=P)).then_inc(v_in[c], 16)

        @block.tensor
        def _(pe):
            pe.sem_inc(scored, SLOTS)
            pe.sem_inc(pv_done, 2 * SLOTS)

            def scores(t, par, s):
                bp, bs = parity(par, s)
                blk = t + s // SLOTS
                g = SLOTS * t + s
                e, c = divmod(bs, KC)
                if bs == 0:
                    pe.wait_ge(q_in[bp], 32 * (blk // 2 + 1))
                if e == 0:
                    pe.wait_ge(k_in[c], 32 * (blk // JB + 1))
                pe.wait_ge(copied, g - 1)
                for k in range(3):
                    for w in range(2):
                        mm = nc.tensor.matmul(psum[:, 3 * (s % 2) + k, 0:CH],
                                              kst[:, e, (3 * c + k) * P:(3 * c + k + 1) * P],
                                              qst[bp][:, 2 * w + e, :], start=(w == 0), stop=(w == 1))
                mm.then_inc(scored, 1)

            def spread_den(t):
                pe.wait_ge(den_copied, t + 1)
                nc.tensor.matmul(den_bank, sel[:, :], den[:, :], start=True, stop=True).then_inc(spread, 1)

            def weigh(t, par, v):
                if v == 0:
                    pe.wait_ge(pv_copied, t)
                for kt in PV_TILES[v]:
                    if kt % 3 == 0:
                        pe.wait_ge(v_in[kt // 3], 16 * (t // JB + 1))
                        pe.wait_ge(exp_done, SLOTS * t + KC + kt // 3 + 1)
                    for e in range(2):
                        mm = nc.tensor.matmul(psum[e * D:(e + 1) * D, 6, 0:CH], vst[:, kt, e * D:(e + 1) * D],
                                              prob[par][:, e, kt, :], start=(kt == 0), stop=(kt == KT - 1))
                if v >= DEN_AT:
                    j = v - DEN_AT
                    if j == 0:
                        pe.wait_ge(spread_copied, t)
                    for e in range(2):
                        for odd in range(2):
                            r = 64 * e + 32 * odd
                            mm = nc.tensor.matmul(psum[r:r + 32, 7, 0:CH], ones[:, :],
                                                  prob[par][:, e, 2 * j + odd, :], start=(j == 0),
                                                  stop=(j == KT // 2 - 1), tile_position=(0, r))
                mm.then_inc(pv_done, 1)

            def body(t, par, n_scores=SLOTS):
                for v in range(SLOTS):
                    if v < n_scores and v == 0:
                        scores(t, par, PV_LAG)
                    if v == 0 and not is_block(t, 0):
                        spread_den(t - 1)
                    weigh(t, par, v)
                    if v < n_scores and v > 0:
                        scores(t, par, PV_LAG + v)

            for s in range(2):
                first_scores(pe, nc, psum, kst, qst, q_in, k_in, s, scored)
            for s in range(2, PV_LAG):
                scores(0, 0, s)
            body(0, 0)
            with pe.Fori(0, (NB - 4) // 2) as it:
                for p in range(2):
                    body(2 * it + 1 + p, 1 - p)
            for t in range(NB - 3, NB):
                body(t, t % 2, n_scores=max(0, min(SLOTS, SLOTS * (NB - t) - PV_LAG)))
            spread_den(NB - 1)

        @block.scalar
        def _(act):
            def copy(t, par, s):
                bp, bs = parity(par, s)
                blk = t + s // SLOTS
                g = SLOTS * t + s
                act.wait_ge(maxed, g + 1)
                act.wait_ge(pv_done, pv_count(blk - 2, LAST_USE[bs % KC]))
                nc.scalar.activation(chunk_of(bp, bs), s_bank(s), ACT.Copy).then_inc(copied, 1)

            def exponential(t, par, s):
                act.wait_ge(dve_shifted, shifted_count(SLOTS * t + s))
                act.wait_ge(pool_shifted, shifted_count(SLOTS * t + s))
                x = chunk_of(par, s)
                nc.scalar.activation(x, x, ACT.Exp, scale=SCALE).then_inc(exp_done, 1)

            def evacuate(t):
                act.wait_ge(pv_done, pv_count(t, SLOTS - 1))
                act.wait_ge(spread, t)
                nc.scalar.activation(den[:, :], den_bank, ACT.Copy).then_inc(den_copied, 1)
                act.wait_ge(normed, t)
                nc.scalar.activation(pvr[:, :], pv_bank, ACT.Copy).then_inc(pv_copied, 1)

            def copy_spread(t):
                act.wait_ge(spread, t + 1)
                act.wait_ge(inverted, PARTS * t)
                nc.scalar.activation(dsp[:, :], den_bank, ACT.Copy).then_inc(spread_copied, 1)

            def store(t, par):
                pair = t // JB
                pair_row, j_off = (pair % PAIRS) * P, (pair // PAIRS) * HW + (t % JB) * CH
                act.wait_ge(normed, t + 1)
                act.dma_start(att_d[bass.ds(pair_row, P), bass.ds(j_off, CH)], ob[par][:, :])\
                    .then_inc(stored[par], 16)

            def body(t, par, n_copies=SLOTS):
                for k in range(SLOTS):
                    if k == PV_LAG - 1 - EXP_LAG and not is_block(t, 0):
                        evacuate(t - 1)
                    if k < n_copies:
                        copy(t, par, EXP_LAG + k)
                    if k == PV_LAG - EXP_LAG and not is_block(t, 0):
                        copy_spread(t - 1)
                    exponential(t, par, k)
                if not is_block(t, 0, 1):
                    store(t - 2, par)

            for s in range(EXP_LAG):
                copy(0, 0, s)
            for t in range(2):
                body(t, t)
            with act.Fori(0, (NB - 4) // 2) as it:
                for p in range(2):
                    body(2 * it + 2 + p, p)
            body(NB - 2, 0)
            body(NB - 1, 1, n_copies=SLOTS - EXP_LAG)
            store(NB - 2, 0)
            evacuate(NB - 1)
            copy_spread(NB - 1)
            store(NB - 1, 1)
            for p in range(2):
                act.wait_ge(stored[p], 16 * (NB // 2))

        @block.gpsimd
        def _(pool):
            pool.sem_inc(pool_shifted, SLOTS)
            with pool.Fori(0, NB // 2) as it:
                for par in range(2):
                    t = 2 * it + par
                    for e in range(2):
                        u = 2 * t + e
                        pool.wait_ge(folded, 2 * (u + 1))
                        pool.wait_ge(dve_shifted, shifted_count(KC * (u - 1) - 1))
                        pool.wait_ge(pool_shifted, shifted_count(KC * (u - 1) - 1))
                        pool.sem_inc(reducing, 1)
                        nc.gpsimd.partition_all_reduce(mx[e][:, :], fold[e][:, :], P, bass.bass_isa.ReduceOp.max)\
                            .then_inc(mx_ready, 1)
                        for c in range(KC):
                            pool.wait_ge(mx_ready, u + 1)
                            pool.wait_ge(copied, SLOTS * t + KC * e + c + 1)
                            shift_part(nc.gpsimd, chunk_of(par, KC * e + c), e, SHIFT_DVE, CH)\
                                .then_inc(pool_shifted, 1)

        @block.vector
        def _(dve):
            def maximum(t, par, s, first_units=False):
                g = SLOTS * t + s
                e, c = divmod(s % SLOTS, KC)
                u = 2 * t + s // KC
                dve.wait_ge(scored, scored_count(g))
                r = run[e]
                if c == 0:
                    if not (first_units and s < SLOTS):
                        dve.wait_ge(folded, 2 * (u - 1))
                    nc.vector.tensor_copy(r[:, :, :], s_bank(s)).then_inc(maxed, 1)
                else:
                    dve.wait_ge(maxed, g)
                    nc.vector.tensor_tensor(r[:, :, :], s_bank(s), r[:, :, :], ALU.max).then_inc(maxed, 1)
                if c == KC - 1:
                    dve.wait_ge(maxed, g + 1)
                    if not (first_units and s < SLOTS):
                        dve.wait_ge(mx_ready, u - 1)
                    nc.vector.tensor_tensor(fold[e][:, :], r[:, 0, :], r[:, 1, :], ALU.max).then_inc(folded, 1)
                    dve.wait_ge(folded, 2 * u + 1)
                    nc.vector.tensor_tensor(fold[e][:, :], fold[e][:, :], r[:, 2, :], ALU.max).then_inc(folded, 1)

            def shift(t, par, s):
                dve.wait_ge(mx_ready, 2 * t + s // KC + 1)
                dve.wait_ge(copied, SLOTS * t + s + 1)
                shift_part(nc.vector, chunk_of(par, s), s // KC, 0, SHIFT_DVE).then_inc(dve_shifted, 1)

            def invert(t, part):
                dve.wait_ge(spread_copied, t + 1)
                dve.wait_ge(normed, t)
                q = slice(part * CH // PARTS, (part + 1) * CH // PARTS)
                nc.vector.reciprocal(rec[:, q], dsp[:, q]).then_inc(inverted, 1)

            def norm(t, par):
                dve.wait_ge(inverted, PARTS * (t + 1))
                dve.wait_ge(pv_copied, t + 1)
                if not is_block(t, 0, 1):
                    dve.wait_ge(stored[par], 16 * (t // 2))
                nc.vector.tensor_tensor(ob[par][:, :], pvr[:, :], rec[:, :], ALU.mult).then_inc(normed, 1)

            def body(t, par, n_max=SLOTS):
                for k in range(SLOTS):
                    if k < n_max:
                        maximum(t, par, EXP_LAG + k, first_units=is_block(t, 0))
                    if not is_block(t, 0, 1):
                        if k in INVERT_AT:
                            invert(t - 2, INVERT_AT.index(k))
                        if k == INVERT_AT[-1] + 1:
                            norm(t - 2, par)
                    shift(t, par, k)

            dve.sem_inc(dve_shifted, SLOTS)
            for s in range(EXP_LAG):
                maximum(0, 0, s, first_units=True)
            for t in range(2):
                body(t, t)
            with dve.Fori(0, (NB - 4) // 2) as it:
                for p in range(2):
                    body(2 * it + 2 + p, p)
            body(NB - 2, 0)
            body(NB - 1, 1, n_max=SLOTS - EXP_LAG)
            for t in (NB - 2, NB - 1):
                for part in range(PARTS):
                    invert(t, part)
                norm(t, t % 2)


def first_scores(pe, nc, psum, kst, qst, q_in, k_in, s, scored):
    if s == 0:
        pe.wait_ge(q_in[0], 32)
    pe.wait_ge(k_in[s], 32)
    for k in range(3):
        for w in range(2):
            mm = nc.tensor.matmul(psum[:, 3 * s + k, 0:CH], kst[:, 0, (3 * s + k) * P:(3 * s + k + 1) * P],
                                  qst[0][:, 2 * w, :], start=(w == 0), stop=(w == 1))
    mm.then_inc(scored, 1)


def program(nc, x, params, qkv_w, qkv_bv, proj_w, w1, w1v, w1e, wout, emb, consts, out):
    def dram(name, shape, dt=F32):
        return nc.dram_tensor(name, shape, dt, kind="Internal").ap()

    qk_d = dram("qk_scratch", (2 * CT, 2, P, T))
    v_d = dram("v_scratch", (T, C))
    att_d = dram("att_scratch", (C, T))
    h_d = dram("h_scratch", (C, T))

    with ExitStack() as ctx:
        const_sb = sb_(ctx, nc, "const_sb", [P, 32 + P + P])
        par_sb = sb_(ctx, nc, "par_sb", [P, 2 * CT + 2 * CT + CT + CT])
        ones, sel, gmat = const_sb[:, 0:32], const_sb[:, 32:32 + P], const_sb[:, 32 + P:32 + 2 * P]
        load_stage(nc, [(const_sb[:, :], consts), (par_sb[:, :], params)])
        par = {"gn_w": par_sb[:, 0:CT], "gn_b": par_sb[:, CT:2 * CT], "qkv_b": par_sb[:, 2 * CT:4 * CT],
               "proj_b": par_sb[:, 4 * CT:5 * CT], "bout": par_sb[:, 5 * CT:6 * CT]}

        def weights(w):
            return w.rearrange("(c p) n -> p c n", p=P)

        def chunk_bufs(c2, stage, out_proj, qkv):
            def two(name, shape):
                return [sb_(c2, nc, f"{name}{i}_{stage}", shape) for i in range(2)]

            return {"xc": two("xc", [P, CT, CH]),
                    "att": two("attc", [P, CT, CH]) if out_proj else None,
                    "res": two("resc", [P, CT, CH]) if out_proj else None,
                    "hl": two("hl", [P, CT, 2, CH]) if qkv else None,
                    "vo": two("vo", [P, TT, C]) if qkv else None}

        def attention(layer):
            with ExitStack() as c2:
                psum = c2.enter_context(nc.psum_tensor(f"psum_att{layer}", [P, 8, 512], F32))

                def two(name, shape, dt=F32):
                    return [sb_(c2, nc, f"{name}{i}_{layer}", shape, dt) for i in range(2)]

                bufs = {"kst": sb_(c2, nc, f"kst_{layer}", [P, 2, HW], F32R), "qst": two("qst", [P, 4, CH], F32R),
                        "vst": sb_(c2, nc, f"vst_{layer}", [P, KT, P]), "prob": two("prob", [P, 2, KT, CH]),
                        "run": two("run", [P, 3, CH]), "fold": two("fold", [P, CH]), "mx": two("mx", [P, CH]),
                        "den": sb_(c2, nc, f"den_{layer}", [P, CH]), "dsp": sb_(c2, nc, f"dsp_{layer}", [P, CH]), "pvr": sb_(c2, nc, f"pvr_{layer}", [P, CH]),
                        "rec": sb_(c2, nc, f"rec_{layer}", [P, CH]), "ob": two("ob", [P, CH]),
                        "ones": ones, "sel": sel}
                attention_stage(nc, f"att{layer}", psum, bufs, qk_d, v_d, att_d)

        with ExitStack() as c1:
            x_sb = sb_(c1, nc, "x_sb", [P, CT, T])
            wq = sb_(c1, nc, "wq0", [P, CT, 3 * C])
            bv = sb_(c1, nc, "bv0", [P, C])
            load_stage(nc, [(wq[:, :, :], weights(qkv_w)), (bv[:, :], qkv_bv.partition_broadcast(P))])
            group_norm_stage(nc, x_sb, par, gmat, x)
            psum = c1.enter_context(nc.psum_tensor("psum_0", [P, 8, 512], F32))
            chunk_stage(nc, "l0", psum, chunk_bufs(c1, "l0", False, True), src=x_sb,
                        qkv={"w": wq[:, :, 0:2 * C], "wv": wq[:, :, 2 * C:3 * C], "bias": par["qkv_b"], "bv": bv,
                             "emb": None, "qk": qk_d, "v": v_d})
        attention(0)
        with ExitStack() as c1:
            wo = sb_(c1, nc, "wo0", [P, CT, C])
            wq = sb_(c1, nc, "wq1", [P, CT, 2 * C])
            wv = sb_(c1, nc, "wv1", [P, CT, C])
            we = sb_(c1, nc, "we1", [P, 2 * C])
            em = sb_(c1, nc, "em1", [P, T])
            load_stage(nc, [(wo[:, :, :], weights(proj_w)), (wq[:, :, :], weights(w1)), (wv[:, :, :], weights(w1v)),
                            (we[:, :], w1e), (em[:, 0:HW], emb), (em[:, HW:T], emb)])
            psum = c1.enter_context(nc.psum_tensor("psum_1", [P, 8, 512], F32))
            chunk_stage(nc, "l1", psum, chunk_bufs(c1, "l1", True, True),
                        out_proj={"w": wo, "bias": par["proj_b"], "att": att_d, "res": x, "dst": h_d},
                        qkv={"w": wq, "wv": wv, "bias": None, "bv": None, "emb": {"w": we, "x": em},
                             "qk": qk_d, "v": v_d})
        attention(1)
        with ExitStack() as c1:
            wo = sb_(c1, nc, "wo1", [P, CT, C])
            load_stage(nc, [(wo[:, :, :], weights(wout))])
            psum = c1.enter_context(nc.psum_tensor("psum_2", [P, 8, 512], F32))
            chunk_stage(nc, "l2", psum, chunk_bufs(c1, "l2", True, False),
                        out_proj={"w": wo, "bias": par["bout"], "att": att_d, "res": h_d, "dst": out})


def position_embedding(np):
    f = np.float32
    n, side = 16, 48
    lx = np.log2(np.maximum(np.arange(side * n), 1).astype(f))
    lx[0] = -2.0
    lx = lx.reshape(side, n).T * np.arange(1, n + 1, dtype=f)[:, None]
    freq = np.stack([np.cos(lx), np.sin(lx)], 1).reshape(2 * n, side, 1)
    xx = np.arange(0, n * side, dtype=f).reshape(side, n).T
    th = (np.arange(n, dtype=f) + f(0.5))[:, None] * xx / f(side * n) * f(6.283185307179586)
    time = np.stack([np.cos(th), np.sin(th)], 1).reshape(2 * n, 1, side)
    e = np.zeros((P, side, side), f)
    e[0:2 * n] = freq
    e[2 * n:4 * n] = time
    return e.reshape(P, side * side)


def constants(np):
    f = np.float32
    sel = np.zeros((P, P), f)
    for e in range(2):
        sel[64 * e, 64 * e:64 * e + 64] = 1
        sel[64 * e + 32, 64 * e:64 * e + 64] = 1
    g = np.kron(np.eye(P // GROUP, dtype=f), np.full((GROUP, GROUP), 1.0 / GROUP, f))
    return np.ascontiguousarray(np.concatenate([np.ones((P, 32), f), sel, g], 1))


def kernel(x, L0_conv_gn_w, L0_conv_gn_b, L0_conv_qkv_w, L0_conv_qkv_b, L0_conv_proj_w, L0_conv_proj_b,
           L1_conv_Wq, L1_conv_Wk, L1_conv_Wv, L1_conv_Wout, L1_conv_bout):
    import numpy as np
    import concourse.bacc as bacc
    from concourse.bass_utils import run_bass_kernel_spmd

    def cols(v):
        return np.asarray(v).reshape(-1, P).T

    qkv_w = np.asarray(L0_conv_qkv_w).reshape(8, D, 3, C).transpose(3, 2, 0, 1).reshape(C, 3 * C)
    qkv_b = np.asarray(L0_conv_qkv_b).reshape(8, D, 3).transpose(2, 0, 1).reshape(3 * C)
    wqk = np.concatenate([np.asarray(L1_conv_Wq), np.asarray(L1_conv_Wk)], 1)
    we = np.zeros((P, 2 * C), np.float32)
    we[0:D] = wqk[C:C + D]
    arrays = {
        "x": np.asarray(x).transpose(1, 0, 2, 3).reshape(C, T),
        "params": np.concatenate([cols(L0_conv_gn_w), cols(L0_conv_gn_b), cols(qkv_b[0:2 * C]),
                                  cols(L0_conv_proj_b), cols(L1_conv_bout)], 1),
        "qkv_w": qkv_w,
        "qkv_bv": qkv_b[2 * C:3 * C],
        "proj_w": np.asarray(L0_conv_proj_w).T,
        "w1": wqk[0:C], "w1v": np.asarray(L1_conv_Wv), "w1e": we,
        "wout": np.asarray(L1_conv_Wout),
        "emb": position_embedding(np),
        "consts": constants(np),
    }
    nc = bacc.Bacc("TRN2", target_bir_lowering=False, num_devices=1)
    arrays = {f"in_{k}": np.ascontiguousarray(v) for k, v in arrays.items()}
    ins = {k[3:]: nc.dram_tensor(k, v.shape, F32, kind="ExternalInput").ap() for k, v in arrays.items()}
    out = nc.dram_tensor("out_y", (C, T), F32, kind="ExternalOutput").ap()
    program(nc, **ins, out=out)
    r = run_bass_kernel_spmd(nc, [arrays], core_ids=[0])
    y = np.asarray(r.results[0]["out_y"])
    return np.ascontiguousarray(y.reshape(C, B, 48, 48).transpose(1, 0, 2, 3))
```

```python
from contextlib import ExitStack

import concourse.bass as bass
from concourse import mybir

F32 = mybir.dt.float32
F32R = mybir.dt.float32r
ALU = mybir.AluOpType
ACT = mybir.ActivationFunctionType
AX = mybir.AxisListType

P = 128
SIDE = 48
B, C, HW = 2, 512, SIDE * SIDE
T = B * HW
CT = C // P
D = 64
PAIRS = C // (2 * D)
GROUP = C // 32
CH = 384
NCH = T // CH
TT = CH // P
KT = HW // P
JB = HW // CH
KC = KT // 3
SLOTS = 2 * KC
NB = B * PAIRS * JB
SCALE = float(D) ** -0.5
GN_EPS = 1e-5
SHIFT_DVE = 208
EXP_LAG = 8
PV_LAG = SLOTS + 5

PV_COUNTS = [2, 2, 2, 2, 1, 2, 1, 1, 2, 1, 1, 1]
PV_TILES = [list(range(sum(PV_COUNTS[:v]), sum(PV_COUNTS[:v + 1]))) for v in range(SLOTS)]
SCORES_FIRST = (0, SLOTS - 1)
DEN_AT = SLOTS - KT // 2
LAST_USE = [max(max(v for v in range(SLOTS) if set(PV_TILES[v]) & {3 * c, 3 * c + 1, 3 * c + 2}),
                DEN_AT + (3 * c + 2) // 2) for c in range(KC)]


INVERT_AT = [0, 1, 2, 4, 5, 6]
PARTS = len(INVERT_AT)


def is_block(t, *numbers):
    return isinstance(t, int) and t in numbers


def sb_(ctx, nc, name, shape, dt=F32):
    return ctx.enter_context(nc.sbuf_tensor(name, shape, dt))


def group_norm_stage(nc, x_sb, aa, bb, par, gmat, x_d, others):
    with ExitStack() as ctx:
        st = sb_(ctx, nc, "gn_stats", [P, B * CT, JB, 6])
        mv = sb_(ctx, nc, "gn_mv", [P, B * CT, 2])
        dif = sb_(ctx, nc, "gn_dif", [P, B * CT])
        vv = sb_(ctx, nc, "gn_var", [P, B * CT])
        sd = sb_(ctx, nc, "gn_sd", [P, B * CT])
        rs = sb_(ctx, nc, "gn_rstd", [P, B * CT])
        tmp = sb_(ctx, nc, "gn_tmp", [P, B * CT])
        pm = ctx.enter_context(nc.psum_tensor("gn_mean", [P, 512], F32))
        pv = ctx.enter_context(nc.psum_tensor("gn_pvar", [P, 512], F32))
        x_in = [ctx.enter_context(nc.semaphore(f"x_in{n}")) for n in range(B * CT)]
        others_in = ctx.enter_context(nc.semaphore("others_in"))
        stats = ctx.enter_context(nc.semaphore("stats"))
        mean_mm = ctx.enter_context(nc.semaphore("mean_mm"))
        var_mm = ctx.enter_context(nc.semaphore("var_mm"))
        dev_done = ctx.enter_context(nc.semaphore("dev_done"))
        var_done = ctx.enter_context(nc.semaphore("var_done"))
        root_done = ctx.enter_context(nc.semaphore("root_done"))
        step = ctx.enter_context(nc.semaphore("gn_step"))
        block = ctx.enter_context(nc.Block())
        N = B * CT

        @block.sync
        def _(sp):
            for n in range(N):
                b, c = divmod(n, CT)
                sp.dma_start(x_sb[:, c, b * HW:(b + 1) * HW],
                             x_d[c * P:(c + 1) * P, b * HW:(b + 1) * HW]).then_inc(x_in[n], 16)
                if n == 0:
                    for dst, src in others:
                        sp.dma_start(dst, src).then_inc(others_in, 16)

        @block.tensor
        def _(pe):
            pe.wait_ge(others_in, 16 * len(others))
            pe.wait_ge(stats, N)
            nc.tensor.matmul(pm[:, 0:N], gmat[:, :], mv[:, :, 0], start=True, stop=True).then_inc(mean_mm, 1)
            pe.wait_ge(dev_done, 1)
            nc.tensor.matmul(pv[:, 0:N], gmat[:, :], vv[:, :], start=True, stop=True).then_inc(var_mm, 1)

        @block.scalar
        def _(act):
            act.wait_ge(var_done, 1)
            nc.scalar.activation(sd[:, :], vv[:, :], ACT.Sqrt).then_inc(root_done, 1)

        @block.vector
        def _(dve):
            done = [0]

            def then(ins):
                done[0] += 1
                ins.then_inc(step, 1)
                return done[0]

            for n in range(N):
                b, c = divmod(n, CT)
                dve.wait_ge(x_in[n], 16)
                for j in range(JB):
                    k = then(nc.vector.bn_stats(st[:, n, j, :], x_sb[:, c, b * HW + j * CH:b * HW + (j + 1) * CH]))
            dve.wait_ge(step, k)
            for n in range(N):
                nc.vector.bn_aggr(mv[:, n, :], st[:, n, :, :]).then_inc(stats, 1)
            dve.wait_ge(stats, N)
            dve.wait_ge(mean_mm, 1)
            k = then(nc.vector.tensor_tensor(dif[:, :], mv[:, :, 0], pm[:, 0:N], ALU.subtract))
            dve.wait_ge(step, k)
            k = then(nc.vector.tensor_tensor(tmp[:, :], dif[:, :], dif[:, :], ALU.mult))
            dve.wait_ge(step, k)
            nc.vector.tensor_tensor(vv[:, :], tmp[:, :], mv[:, :, 1], ALU.add).then_inc(dev_done, 1)
            dve.wait_ge(var_mm, 1)
            nc.vector.tensor_scalar(vv[:, :], pv[:, 0:N], GN_EPS, None, ALU.add).then_inc(var_done, 1)
            dve.wait_ge(root_done, 1)
            k = then(nc.vector.reciprocal(rs[:, :], sd[:, :]))
            dve.wait_ge(step, k)
            k = then(nc.vector.tensor_tensor(tmp[:, :], rs[:, :], rs[:, :], ALU.mult))
            dve.wait_ge(step, k)
            dve.wait_ge(var_done, 1)
            k = then(nc.vector.tensor_tensor(tmp[:, :], tmp[:, :], vv[:, :], ALU.mult))
            dve.wait_ge(step, k)
            k = then(nc.vector.tensor_scalar(tmp[:, :], tmp[:, :], -0.5, 1.5, ALU.mult, ALU.add))
            dve.wait_ge(step, k)
            k = then(nc.vector.tensor_tensor(rs[:, :], rs[:, :], tmp[:, :], ALU.mult))
            dve.wait_ge(step, k)
            for b in range(B):
                s = slice(b * CT, (b + 1) * CT)
                k = then(nc.vector.tensor_tensor(aa[:, s], rs[:, s], par["gn_w"], ALU.mult))
            dve.wait_ge(step, k)
            k = then(nc.vector.tensor_tensor(tmp[:, :], aa[:, :], pm[:, 0:N], ALU.mult))
            dve.wait_ge(step, k)
            for b in range(B):
                s = slice(b * CT, (b + 1) * CT)
                k = then(nc.vector.tensor_tensor(bb[:, s], par["gn_b"], tmp[:, s], ALU.subtract))


def out_projection(nc, bank, w, att):
    for c in range(CT):
        mm = nc.tensor.matmul(bank, w[c], att[:, c, :], start=(c == 0), stop=(c == CT - 1))
    return mm


def qkv_stage(nc, name, psum, bufs, weights, qkv, norm=None, out_proj=None):
    with ExitStack() as ctx:
        def sem(n):
            return ctx.enter_context(nc.semaphore(f"{name}_{n}"))

        xc, att, res, hl, vo = bufs["xc"], bufs["att"], bufs["res"], bufs["hl"], bufs["vo"]
        emb, bias, bv = qkv["emb"], qkv["bias"], qkv["bv"]
        w_in = [sem(f"w_in{n}") for n in range(len(weights))]
        att_in = [sem(f"att_in{p}") for p in range(2)]
        res_in = [sem(f"res_in{p}") for p in range(2)]
        xc_ready = sem("xc_ready")
        out_mm = sem("out_mm")
        qk_mm = sem("qk_mm")
        v_mm = sem("v_mm")
        summed = sem("summed")
        high_done = sem("high_done")
        low_done = sem("low_done")
        v_done = sem("v_done")
        q_stored, k_stored = sem("q_stored"), sem("k_stored")
        v_stored = [sem(f"v_stored{p}") for p in range(2)]
        x_stored = [sem(f"x_stored{p}") for p in range(2)]
        emb_mm, emb_copied = sem("emb_mm"), sem("emb_copied")
        emb_dve, emb_pool = sem("emb_dve"), sem("emb_pool")
        block = ctx.enter_context(nc.Block())
        MT = 2 * CT

        def qk_bank(m):
            return psum[:, m % 4, 0:CH]

        def v_bank(p, tt):
            return psum[:, 4 + (TT * p + tt) % 2, 0:C]

        def out_bank(m):
            return psum[:, 6 + m % 2, 0:CH]

        def tokens(i):
            return bass.ds(i * CH, CH)

        def pairs_of_chunks(engine, pair):
            pair(0, False)
            with engine.Fori(1, NCH // 2 - 1) as it:
                pair(it, False)
            pair(NCH // 2 - 1, True)

        def add_embedding(engine, m):
            rows = bufs["emb_parts"][:, m, 0:SIDE].unsqueeze(2).broadcast_to([P, SIDE, SIDE])
            cols = bufs["emb_parts"][:, m, SIDE:2 * SIDE].unsqueeze(1).broadcast_to([P, SIDE, SIDE])
            return engine.tensor_tensor(bufs["emb_table"][:, m, :].rearrange("p (h w) -> p h w", h=SIDE),
                                        rows, cols, ALU.add)

        @block.sync
        def _(sp):
            def load_att(i, p):
                sp.dma_start(att[p][:, :, :], out_proj["att"].rearrange("(c p) t -> p c t", p=P)[:, :, tokens(i)])\
                    .then_inc(att_in[p], 16)

            def load_res(i, p):
                sp.dma_start(res[p][:, :, :], out_proj["res"].rearrange("(c p) t -> p c t", p=P)[:, :, tokens(i)])\
                    .then_inc(res_in[p], 16)

            for n, (dst, src) in enumerate(weights):
                if out_proj and n == out_proj["loads_at"]:
                    load_att(0, 0)
                    load_res(0, 0)
                sp.dma_start(dst, src).then_inc(w_in[n], 16)
            if out_proj:
                load_att(1, 1)
                load_res(1, 1)

            def pair(it, last):
                for p in range(2):
                    i = 2 * it + p
                    if out_proj:
                        if not last:
                            sp.wait_ge(out_mm, CT * (i + 1))
                            load_att(i + 2, p)
                        sp.wait_ge(xc_ready, CT * (i + 1))
                        if not last:
                            load_res(i + 2, p)
                        sp.dma_start(out_proj["dst"].rearrange("(c p) t -> p c t", p=P)[:, :, tokens(i)],
                                     xc[p][:, :, :]).then_inc(x_stored[p], 16)
                    for half, stored in ((0, q_stored), (1, k_stored)):
                        sp.wait_ge(low_done, MT * i + CT * (half + 1))
                        sp.dma_start(qkv["qk"].rearrange("m w p t -> p (m w) t")[:, half * MT:(half + 1) * MT, tokens(i)],
                                     hl[half].rearrange("p m w t -> p (m w) t")).then_inc(stored, 16)
                    sp.wait_ge(v_done, TT * (i + 1))
                    sp.dma_start(qkv["v"][tokens(i), :].rearrange("(a p) d -> p a d", p=P),
                                 vo[p][:, :, :]).then_inc(v_stored[p], 16)

            pairs_of_chunks(sp, pair)
            for p in range(2):
                if out_proj:
                    sp.wait_ge(x_stored[p], 16 * (NCH // 2))
                sp.wait_ge(v_stored[p], 16 * (NCH // 2))
            sp.wait_ge(q_stored, 16 * NCH)
            sp.wait_ge(k_stored, 16 * NCH)

        @block.tensor
        def _(pe):
            def out_tiles(i, p):
                pe.wait_ge(att_in[p], 16 * (i // 2 + 1))
                for m in range(CT):
                    if m >= 2:
                        pe.wait_ge(xc_ready, CT * i + m - 1)
                    elif m == 0 and not is_block(i, 0):
                        pe.wait_ge(xc_ready, CT * i)
                    w = [out_proj["w"][:, c, m * P:(m + 1) * P] for c in range(CT)]
                    out_projection(nc, out_bank(m), w, att[p]).then_inc(out_mm, 1)

            if emb:
                pe.wait_ge(w_in[emb["w_at"]], 16)
                pe.wait_ge(w_in[emb["x_at"]], 16)
                for m in range(MT):
                    mm = nc.tensor.matmul(psum[:, 4 + m // 4, (m % 4) * P:(m % 4) * P + 2 * SIDE],
                                          emb["w"][:, m * P:(m + 1) * P], emb["x"][:, :], start=True, stop=True)
                mm.then_inc(emb_mm, 1)
            if out_proj:
                pe.wait_ge(w_in[out_proj["w_at"]], 16)
                out_tiles(0, 0)
            pe.wait_ge(w_in[qkv["w_at"]], 16)

            def pair(it, last):
                for p in range(2):
                    i = 2 * it + p
                    pe.wait_ge(xc_ready, CT * (i + 1))
                    for m in range(MT):
                        if m >= 4:
                            pe.wait_ge(low_done, MT * i + m - 3)
                        elif m == 0 and not is_block(i, 0):
                            pe.wait_ge(low_done, MT * i)
                        for c in range(CT):
                            mm = nc.tensor.matmul(qk_bank(m), qkv["w"][:, c, m * P:(m + 1) * P], xc[p][:, c, :],
                                                  start=(c == 0), stop=(c == CT - 1))
                        mm.then_inc(qk_mm, 1)
                    if out_proj and not (last and p == 1):
                        out_tiles(i + 1, 1 - p)
                    if is_block(i, 0):
                        pe.wait_ge(w_in[qkv["wv_at"]], 16)
                        if emb:
                            pe.wait_ge(emb_copied, 1)
                    for tt in range(TT):
                        if tt >= 2:
                            pe.wait_ge(v_done, TT * i + tt - 1)
                        elif tt == 0 and not is_block(i, 0):
                            pe.wait_ge(v_done, TT * i)
                        for c in range(CT):
                            mm = nc.tensor.matmul(v_bank(p, tt), xc[p][:, c, tt * P:(tt + 1) * P], qkv["wv"][:, c, :],
                                                  start=(c == 0), stop=(c == CT - 1))
                        mm.then_inc(v_mm, 1)

            pairs_of_chunks(pe, pair)

        @block.scalar
        def _(act):
            if emb:
                act.wait_ge(emb_mm, 1)
                nc.scalar.activation(bufs["emb_parts"][:, :, :].rearrange("p (a m) t -> p a m t", a=2),
                                     psum[:, 4:6, :].rearrange("p a (m t) -> p a m t", m=4)[:, :, :, 0:2 * SIDE],
                                     ACT.Copy).then_inc(emb_copied, 1)

            def pair(it, last):
                for p in range(2):
                    i = 2 * it + p
                    for m in range(MT):
                        half, mt = divmod(m, CT)
                        if mt == 0 and not is_block(i, 0):
                            act.wait_ge((q_stored, k_stored)[half], 16 * i)
                        high = hl[half][:, mt, 0, :].bitcast(F32R)
                        if emb:
                            act.wait_ge(summed, MT * i + m + 1)
                            a = nc.scalar.activation(high, bufs["sum"][m % 2][:, :], ACT.Copy)
                        else:
                            act.wait_ge(qk_mm, MT * i + m + 1)
                            a = nc.scalar.activation(high, qk_bank(m), ACT.Identity, bias=bias[:, m:m + 1])
                        a.then_inc(high_done, 1)

            pairs_of_chunks(act, pair)

        @block.gpsimd
        def _(pool):
            if emb:
                pool.wait_ge(emb_copied, 1)
                for m in range(1, MT, 2):
                    add_embedding(nc.gpsimd, m).then_inc(emb_pool, 1)

        @block.vector
        def _(dve):
            def input_chunk(i, p):
                if out_proj:
                    dve.wait_ge(res_in[p], 16 * (i // 2 + 1))
                if not is_block(i, 0, 1):
                    if out_proj:
                        dve.wait_ge(x_stored[p], 16 * (i // 2))
                    dve.wait_ge(v_mm, TT * (i - 1))
                for c in range(CT):
                    if out_proj:
                        dve.wait_ge(out_mm, CT * i + c + 1)
                        d = nc.vector.scalar_tensor_tensor(out=xc[p][:, c, :], in0=out_bank(c),
                                                           scalar=out_proj["bias"][:, c:c + 1], in1=res[p][:, c, :],
                                                           op0=ALU.add, op1=ALU.add)
                    else:
                        n = bass.ds(i // JB * CT + c, 1)
                        d = nc.vector.tensor_scalar(xc[p][:, c, :], norm["x"][:, c, tokens(i)], norm["scale"][:, n],
                                                    norm["shift"][:, n], ALU.mult, ALU.add)
                    d.then_inc(xc_ready, 1)

            if emb:
                dve.wait_ge(emb_copied, 1)
                for m in range(0, MT, 2):
                    if m == 2:
                        input_chunk(0, 0)
                    add_embedding(nc.vector, m).then_inc(emb_dve, 1)
            else:
                input_chunk(0, 0)

            def pair(it, last):
                for p in range(2):
                    i = 2 * it + p
                    for m in range(MT):
                        half, mt = divmod(m, CT)
                        high, low = hl[half][:, mt, 0, :], hl[half][:, mt, 1, :].bitcast(F32R)
                        if emb:
                            if is_block(i, 0):
                                dve.wait_ge((emb_dve, emb_pool)[m % 2], m // 2 + 1)
                            dve.wait_ge(qk_mm, MT * i + m + 1)
                            if not (is_block(i, 0) and m < 2):
                                dve.wait_ge(low_done, MT * i + m - 1)
                            nc.vector.tensor_tensor(bufs["sum"][m % 2][:, :], qk_bank(m),
                                                    emb_of(i, m), ALU.add).then_inc(summed, 1)
                            dve.wait_ge(high_done, MT * i + m + 1)
                            nc.vector.tensor_tensor(low, bufs["sum"][m % 2][:, :], high, ALU.subtract)\
                                .then_inc(low_done, 1)
                        else:
                            dve.wait_ge(high_done, MT * i + m + 1)
                            nc.vector.scalar_tensor_tensor(out=low, in0=qk_bank(m), scalar=bias[:, m:m + 1], in1=high,
                                                           op0=ALU.add, op1=ALU.subtract).then_inc(low_done, 1)
                    if not (last and p == 1):
                        input_chunk(i + 1, 1 - p)
                    for tt in range(TT):
                        if tt == 0 and not is_block(i, 0, 1):
                            dve.wait_ge(v_stored[p], 16 * it)
                        dve.wait_ge(v_mm, TT * i + tt + 1)
                        if bv is not None and is_block(i, 0):
                            dve.wait_ge(w_in[qkv["bv_at"]], 16)
                        if bv is not None:
                            d = nc.vector.tensor_tensor(vo[p][:, tt, :], v_bank(p, tt), bv[:, :], ALU.add)
                        else:
                            d = nc.vector.tensor_copy(vo[p][:, tt, :], v_bank(p, tt))
                        d.then_inc(v_done, 1)

            def emb_of(i, m):
                return bufs["emb_table"][:, m, bass.ds(i % JB * CH, CH)]

            pairs_of_chunks(dve, pair)


def output_stage(nc, name, psum, bufs, w, weights, bias, att_d, res_d, out_d):
    with ExitStack() as ctx:
        def sem(n):
            return ctx.enter_context(nc.semaphore(f"{name}_{n}"))

        xc, att, res = bufs["xc"], bufs["att"], bufs["res"]
        w_in = sem("w_in")
        att_in = [sem(f"att_in{p}") for p in range(2)]
        res_in = [sem(f"res_in{p}") for p in range(2)]
        out_mm, summed = sem("out_mm"), sem("summed")
        stored = [sem(f"stored{p}") for p in range(2)]
        block = ctx.enter_context(nc.Block())

        def rows(d, i):
            return d.rearrange("(c p) t -> p c t", p=P)[:, :, bass.ds(i * CH, CH)]

        def bank(p, m):
            return psum[:, CT * p + m, 0:CH]

        @block.sync
        def _(sp):
            sp.dma_start(att[0][:, :, :], rows(att_d, 0)).then_inc(att_in[0], 16)
            sp.dma_start(w[:, :, :], weights).then_inc(w_in, 16)
            sp.dma_start(res[0][:, :, :], rows(res_d, 0)).then_inc(res_in[0], 16)
            sp.dma_start(att[1][:, :, :], rows(att_d, 1)).then_inc(att_in[1], 16)
            sp.dma_start(res[1][:, :, :], rows(res_d, 1)).then_inc(res_in[1], 16)
            with sp.Fori(0, NCH // 2 - 1) as it:
                for p in range(2):
                    i = 2 * it + p
                    sp.wait_ge(out_mm, CT * (i + 1))
                    sp.dma_start(att[p][:, :, :], rows(att_d, i + 2)).then_inc(att_in[p], 16)
                    sp.wait_ge(summed, CT * (i + 1))
                    sp.dma_start(res[p][:, :, :], rows(res_d, i + 2)).then_inc(res_in[p], 16)

        @block.scalar
        def _(act):
            with act.Fori(0, NCH // 2) as it:
                for p in range(2):
                    act.wait_ge(summed, CT * (2 * it + p + 1))
                    act.dma_start(rows(out_d, 2 * it + p), xc[p][:, :, :]).then_inc(stored[p], 16)
            for p in range(2):
                act.wait_ge(stored[p], 16 * (NCH // 2))

        @block.tensor
        def _(pe):
            pe.wait_ge(w_in, 16)

            def pair(it):
                for p in range(2):
                    i = 2 * it + p
                    pe.wait_ge(att_in[p], 16 * (it + 1))
                    if not is_block(i, 0, 1):
                        pe.wait_ge(summed, CT * (i - 1))
                    for m in range(CT):
                        out_projection(nc, bank(p, m), [w[:, c, m * P:(m + 1) * P] for c in range(CT)], att[p])\
                            .then_inc(out_mm, 1)

            pair(0)
            with pe.Fori(1, NCH // 2) as it:
                pair(it)

        @block.vector
        def _(dve):
            def pair(it):
                for p in range(2):
                    i = 2 * it + p
                    dve.wait_ge(res_in[p], 16 * (it + 1))
                    if not is_block(i, 0, 1):
                        dve.wait_ge(stored[p], 16 * it)
                    for m in range(CT):
                        dve.wait_ge(out_mm, CT * i + m + 1)
                        nc.vector.scalar_tensor_tensor(out=xc[p][:, m, :], in0=bank(p, m), scalar=bias[:, m:m + 1],
                                                       in1=res[p][:, m, :], op0=ALU.add, op1=ALU.add)\
                            .then_inc(summed, 1)

            pair(0)
            with dve.Fori(1, NCH // 2) as it:
                pair(it)


def attention_stage(nc, name, psum, bufs, qk_d, v_d, att_d):
    with ExitStack() as ctx:
        def sem(n):
            return ctx.enter_context(nc.semaphore(f"{name}_{n}"))

        kst, qst, vst, prob = bufs["kst"], bufs["qst"], bufs["vst"], bufs["prob"]
        run, fold, mx = bufs["run"], bufs["fold"], bufs["mx"]
        den, dsp, pvr, rec, ob = bufs["den"], bufs["dsp"], bufs["pvr"], bufs["rec"], bufs["ob"]
        ones, sel = bufs["ones"], bufs["sel"]
        q_in = [sem(f"q_in{p}") for p in range(2)]
        k_in = [sem(f"k_in{c}") for c in range(KC)]
        v_in = [sem(f"v_in{c}") for c in range(KC)]
        scored = sem("scored")
        copied = sem("copied")
        maxed = sem("maxed")
        folded = sem("folded")
        reducing = sem("reducing")
        mx_ready = sem("mx_ready")
        dve_shifted, pool_shifted = sem("dve_shifted"), sem("pool_shifted")
        exp_done = sem("exp_done")
        pv_done = sem("pv_done")
        den_copied, pv_copied = sem("den_copied"), sem("pv_copied")
        spread = sem("spread")
        spread_copied = sem("spread_copied")
        inverted = sem("inverted")
        normed = sem("normed")
        stored = [sem(f"stored{p}") for p in range(2)]
        block = ctx.enter_context(nc.Block())

        def scored_count(g):
            return SLOTS + g + 1

        def pv_count(t, v):
            return 2 * SLOTS + SLOTS * t + v + 1

        def shifted_count(g):
            return SLOTS + g + 1

        def maxed_count(t, s):
            return (SLOTS - 2) * t + s - s // KC

        def s_bank(g):
            return psum[:, 3 * (g % 2):3 * (g % 2) + 3, 0:CH]

        pv_bank = psum[:, 6, 0:CH]
        den_bank = psum[:, 7, 0:CH]

        def chunk_of(par, s):
            e, c = divmod(s, KC)
            return prob[par][:, e, 3 * c:3 * c + 3, :]

        def parity(par, s):
            return (par + s // SLOTS) % 2, s % SLOTS

        def shift_part(engine, x, e, q0, q1):
            return engine.tensor_tensor(x[:, :, q0:q1], x[:, :, q0:q1],
                                        mx[e][:, q0:q1].unsqueeze(1).broadcast_to([P, 3, q1 - q0]), ALU.subtract)

        @block.sync
        def _(sp):
            with sp.Fori(0, B) as b, sp.Fori(0, PAIRS) as hp:
                pair = b * PAIRS + hp
                for j in range(JB):
                    t = pair * JB + j
                    sp.wait_ge(scored, scored_count(SLOTS * t - SLOTS - 1))
                    for half in range(2):
                        sp.dma_start(
                            qst[j % 2][half * D:(half + 1) * D, :, :].bitcast(F32),
                            qk_d[bass.ds(hp, 1), :, :, bass.ds(b * HW + j * CH, CH)]
                            .rearrange("m w (e p) t -> p (m w e) t", e=2)).then_inc(q_in[j % 2], 16)
                    if j == 0:
                        for c in range(KC):
                            sp.wait_ge(scored, scored_count(SLOTS * (t - 1) + KC + c))
                            for w in range(2):
                                sp.dma_start(
                                    kst[w * D:(w + 1) * D, :, c * CH:(c + 1) * CH].bitcast(F32),
                                    qk_d[bass.ds(PAIRS + hp, 1), w, :, bass.ds(b * HW + c * CH, CH)]
                                    .rearrange("m (e p) t -> p (m e) t", e=2)).then_inc(k_in[c], 16)
                    if j == 1:
                        for c in range(KC):
                            sp.wait_ge(pv_done, pv_count(t - 2, LAST_USE[c]))
                            sp.dma_start(
                                vst[:, 3 * c:3 * c + 3, :],
                                v_d[bass.ds(b * HW + c * CH, CH), bass.ds(hp * P, P)]
                                .rearrange("(a p) d -> p a d", p=P)).then_inc(v_in[c], 16)

        @block.tensor
        def _(pe):
            pe.sem_inc(scored, SLOTS)
            pe.sem_inc(pv_done, 2 * SLOTS)

            def scores(t, par, s):
                bp, bs = parity(par, s)
                blk = t + s // SLOTS
                g = SLOTS * t + s
                e, c = divmod(bs, KC)
                if bs == 0:
                    pe.wait_ge(q_in[bp], 32 * (blk // 2 + 1))
                if e == 0:
                    pe.wait_ge(k_in[c], 32 * (blk // JB + 1))
                pe.wait_ge(copied, g - 1)
                for k in range(3):
                    for w in range(2):
                        mm = nc.tensor.matmul(psum[:, 3 * (s % 2) + k, 0:CH],
                                              kst[:, e, (3 * c + k) * P:(3 * c + k + 1) * P],
                                              qst[bp][:, 2 * w + e, :], start=(w == 0), stop=(w == 1))
                mm.then_inc(scored, 1)

            def spread_den(t):
                pe.wait_ge(den_copied, t + 1)
                nc.tensor.matmul(den_bank, sel[:, :], den[:, :], start=True, stop=True).then_inc(spread, 1)

            def weigh(t, par, v):
                if v == 0:
                    pe.wait_ge(pv_copied, t)
                for kt in PV_TILES[v]:
                    if kt % 3 == 0:
                        pe.wait_ge(v_in[kt // 3], 16 * (t // JB + 1))
                        pe.wait_ge(exp_done, SLOTS * t + KC + kt // 3 + 1)
                    for e in range(2):
                        mm = nc.tensor.matmul(psum[e * D:(e + 1) * D, 6, 0:CH], vst[:, kt, e * D:(e + 1) * D],
                                              prob[par][:, e, kt, :], start=(kt == 0), stop=(kt == KT - 1))
                if v >= DEN_AT:
                    j = v - DEN_AT
                    if j == 0:
                        pe.wait_ge(spread_copied, t)
                    for e in range(2):
                        for odd in range(2):
                            r = 64 * e + 32 * odd
                            mm = nc.tensor.matmul(psum[r:r + 32, 7, 0:CH], ones[:, :],
                                                  prob[par][:, e, 2 * j + odd, :], start=(j == 0),
                                                  stop=(j == KT // 2 - 1), tile_position=(0, r))
                mm.then_inc(pv_done, 1)

            def body(t, par, n_scores=SLOTS):
                for v in range(SLOTS):
                    if v < n_scores and v in SCORES_FIRST:
                        scores(t, par, PV_LAG + v)
                    if v == 0 and not is_block(t, 0):
                        spread_den(t - 1)
                    weigh(t, par, v)
                    if v < n_scores and v not in SCORES_FIRST:
                        scores(t, par, PV_LAG + v)

            for s in range(2):
                first_scores(pe, nc, psum, kst, qst, q_in, k_in, s, scored)
            for s in range(2, PV_LAG):
                scores(0, 0, s)
            body(0, 0)
            with pe.Fori(0, (NB - 4) // 2) as it:
                for p in range(2):
                    body(2 * it + 1 + p, 1 - p)
            for t in range(NB - 3, NB):
                body(t, t % 2, n_scores=max(0, min(SLOTS, SLOTS * (NB - t) - PV_LAG)))
            spread_den(NB - 1)

        @block.scalar
        def _(act):
            def copy(t, par, s):
                bp, bs = parity(par, s)
                blk = t + s // SLOTS
                g = SLOTS * t + s
                if bs % KC == 0:
                    act.wait_ge(scored, scored_count(g))
                else:
                    act.wait_ge(maxed, maxed_count(blk, bs))
                act.wait_ge(pv_done, pv_count(blk - 2, LAST_USE[bs % KC]))
                nc.scalar.activation(chunk_of(bp, bs), s_bank(s), ACT.Copy).then_inc(copied, 1)

            def exponential(t, par, s):
                act.wait_ge(dve_shifted, shifted_count(SLOTS * t + s))
                act.wait_ge(pool_shifted, shifted_count(SLOTS * t + s))
                x = chunk_of(par, s)
                nc.scalar.activation(x, x, ACT.Exp, scale=SCALE).then_inc(exp_done, 1)

            def evacuate(t):
                act.wait_ge(pv_done, pv_count(t, SLOTS - 1))
                act.wait_ge(spread, t)
                nc.scalar.activation(den[:, :], den_bank, ACT.Copy).then_inc(den_copied, 1)
                act.wait_ge(normed, t)
                nc.scalar.activation(pvr[:, :], pv_bank, ACT.Copy).then_inc(pv_copied, 1)

            def copy_spread(t):
                act.wait_ge(spread, t + 1)
                act.wait_ge(inverted, PARTS * t)
                nc.scalar.activation(dsp[:, :], den_bank, ACT.Copy).then_inc(spread_copied, 1)

            def store(t, par):
                pair = t // JB
                pair_row, j_off = (pair % PAIRS) * P, (pair // PAIRS) * HW + (t % JB) * CH
                act.wait_ge(normed, t + 1)
                act.dma_start(att_d[bass.ds(pair_row, P), bass.ds(j_off, CH)], ob[par][:, :])\
                    .then_inc(stored[par], 16)

            def body(t, par, n_copies=SLOTS):
                for k in range(SLOTS):
                    if k < n_copies:
                        copy(t, par, EXP_LAG + k)
                    if k == PV_LAG - 2 - EXP_LAG and not is_block(t, 0):
                        evacuate(t - 1)
                    if k == PV_LAG - EXP_LAG and not is_block(t, 0):
                        copy_spread(t - 1)
                    exponential(t, par, k)
                if not is_block(t, 0, 1):
                    store(t - 2, par)

            for s in range(EXP_LAG):
                copy(0, 0, s)
            for t in range(2):
                body(t, t)
            with act.Fori(0, (NB - 4) // 2) as it:
                for p in range(2):
                    body(2 * it + 2 + p, p)
            body(NB - 2, 0)
            body(NB - 1, 1, n_copies=SLOTS - EXP_LAG)
            store(NB - 2, 0)
            evacuate(NB - 1)
            copy_spread(NB - 1)
            store(NB - 1, 1)
            for p in range(2):
                act.wait_ge(stored[p], 16 * (NB // 2))

        @block.gpsimd
        def _(pool):
            pool.sem_inc(pool_shifted, SLOTS)
            with pool.Fori(0, NB // 2) as it:
                for par in range(2):
                    t = 2 * it + par
                    for e in range(2):
                        u = 2 * t + e
                        pool.wait_ge(folded, 2 * (u + 1))
                        pool.wait_ge(dve_shifted, shifted_count(KC * (u - 1) - 1))
                        pool.wait_ge(pool_shifted, shifted_count(KC * (u - 1) - 1))
                        pool.sem_inc(reducing, 1)
                        nc.gpsimd.partition_all_reduce(mx[e][:, :], fold[e][:, :], P, bass.bass_isa.ReduceOp.max)\
                            .then_inc(mx_ready, 1)
                        for c in range(KC):
                            pool.wait_ge(mx_ready, u + 1)
                            pool.wait_ge(copied, SLOTS * t + KC * e + c + 1)
                            shift_part(nc.gpsimd, chunk_of(par, KC * e + c), e, SHIFT_DVE, CH)\
                                .then_inc(pool_shifted, 1)

        @block.vector
        def _(dve):
            def maximum(t, par, s, first_units=False):
                g = SLOTS * t + s
                bp, bs = parity(par, s)
                e, c = divmod(bs, KC)
                u = 2 * t + s // KC
                if c == 0:
                    return
                r = run[e]
                dve.wait_ge(scored, scored_count(g))
                before = maxed_count(t + s // SLOTS, bs) - 1
                if c == 1:
                    dve.wait_ge(copied, g)
                    if not (first_units and s < SLOTS):
                        dve.wait_ge(folded, 2 * (u - 1))
                    other = chunk_of(bp, bs - 1)
                else:
                    dve.wait_ge(maxed, before)
                    other = r[:, :, :]
                nc.vector.tensor_tensor(r[:, :, :], s_bank(s), other, ALU.max).then_inc(maxed, 1)
                if c == KC - 1:
                    dve.wait_ge(maxed, before + 1)
                    if not (first_units and s < SLOTS):
                        dve.wait_ge(mx_ready, u - 1)
                    nc.vector.tensor_tensor(fold[e][:, :], r[:, 0, :], r[:, 1, :], ALU.max).then_inc(folded, 1)
                    dve.wait_ge(folded, 2 * u + 1)
                    nc.vector.tensor_tensor(fold[e][:, :], fold[e][:, :], r[:, 2, :], ALU.max).then_inc(folded, 1)

            def shift(t, par, s):
                dve.wait_ge(mx_ready, 2 * t + s // KC + 1)
                dve.wait_ge(copied, SLOTS * t + s + 1)
                shift_part(nc.vector, chunk_of(par, s), s // KC, 0, SHIFT_DVE).then_inc(dve_shifted, 1)

            def invert(t, part):
                dve.wait_ge(spread_copied, t + 1)
                dve.wait_ge(normed, t)
                q = slice(part * CH // PARTS, (part + 1) * CH // PARTS)
                nc.vector.reciprocal(rec[:, q], dsp[:, q]).then_inc(inverted, 1)

            def norm(t, par):
                dve.wait_ge(inverted, PARTS * (t + 1))
                dve.wait_ge(pv_copied, t + 1)
                if not is_block(t, 0, 1):
                    dve.wait_ge(stored[par], 16 * (t // 2))
                nc.vector.tensor_tensor(ob[par][:, :], pvr[:, :], rec[:, :], ALU.mult).then_inc(normed, 1)

            def body(t, par, n_max=SLOTS):
                for k in range(SLOTS):
                    if k < n_max:
                        maximum(t, par, EXP_LAG + k, first_units=is_block(t, 0))
                    if not is_block(t, 0, 1):
                        if k in INVERT_AT:
                            invert(t - 2, INVERT_AT.index(k))
                        if k == INVERT_AT[-1] + 1:
                            norm(t - 2, par)
                    shift(t, par, k)

            dve.sem_inc(dve_shifted, SLOTS)
            for s in range(EXP_LAG):
                maximum(0, 0, s, first_units=True)
            for t in range(2):
                body(t, t)
            with dve.Fori(0, (NB - 4) // 2) as it:
                for p in range(2):
                    body(2 * it + 2 + p, p)
            body(NB - 2, 0)
            body(NB - 1, 1, n_max=SLOTS - EXP_LAG)
            for t in (NB - 2, NB - 1):
                for part in range(PARTS):
                    invert(t, part)
                norm(t, t % 2)


def first_scores(pe, nc, psum, kst, qst, q_in, k_in, s, scored):
    if s == 0:
        pe.wait_ge(q_in[0], 32)
    pe.wait_ge(k_in[s], 32)
    for k in range(3):
        for w in range(2):
            mm = nc.tensor.matmul(psum[:, 3 * s + k, 0:CH], kst[:, 0, (3 * s + k) * P:(3 * s + k + 1) * P],
                                  qst[0][:, 2 * w, :], start=(w == 0), stop=(w == 1))
    mm.then_inc(scored, 1)


def program(nc, x, params, qkv_w, qkv_bv, proj_w, w1, w1v, w1e, wout, emb, consts, out):
    def dram(name, shape, dt=F32):
        return nc.dram_tensor(name, shape, dt, kind="Internal").ap()

    qk_d = dram("qk_scratch", (2 * CT, 2, P, T))
    v_d = dram("v_scratch", (T, C))
    att_d = dram("att_scratch", (C, T))
    h_d = dram("h_scratch", (C, T))

    with ExitStack() as ctx:
        const_sb = sb_(ctx, nc, "const_sb", [P, 32 + P + P])
        par_sb = sb_(ctx, nc, "par_sb", [P, 2 * CT + 2 * CT + CT + CT])
        ones, sel, gmat = const_sb[:, 0:32], const_sb[:, 32:32 + P], const_sb[:, 32 + P:32 + 2 * P]
        par = {"gn_w": par_sb[:, 0:CT], "gn_b": par_sb[:, CT:2 * CT], "qkv_b": par_sb[:, 2 * CT:4 * CT],
               "proj_b": par_sb[:, 4 * CT:5 * CT], "bout": par_sb[:, 5 * CT:6 * CT]}

        def weights(w):
            return w.rearrange("(c p) n -> p c n", p=P)

        def chunk_bufs(c2, stage, out_proj, qkv):
            def two(name, shape):
                return [sb_(c2, nc, f"{name}{i}_{stage}", shape) for i in range(2)]

            return {"xc": two("xc", [P, CT, CH]),
                    "att": two("attc", [P, CT, CH]) if out_proj else None,
                    "res": two("resc", [P, CT, CH]) if out_proj else None,
                    "hl": two("hl", [P, CT, 2, CH]) if qkv else None,
                    "vo": two("vo", [P, TT, C]) if qkv else None}

        def attention(layer):
            with ExitStack() as c2:
                psum = c2.enter_context(nc.psum_tensor(f"psum_att{layer}", [P, 8, 512], F32))

                def two(name, shape, dt=F32):
                    return [sb_(c2, nc, f"{name}{i}_{layer}", shape, dt) for i in range(2)]

                bufs = {"kst": sb_(c2, nc, f"kst_{layer}", [P, 2, HW], F32R), "qst": two("qst", [P, 4, CH], F32R),
                        "vst": sb_(c2, nc, f"vst_{layer}", [P, KT, P]), "prob": two("prob", [P, 2, KT, CH]),
                        "run": two("run", [P, 3, CH]), "fold": two("fold", [P, CH]), "mx": two("mx", [P, CH]),
                        "den": sb_(c2, nc, f"den_{layer}", [P, CH]), "dsp": sb_(c2, nc, f"dsp_{layer}", [P, CH]), "pvr": sb_(c2, nc, f"pvr_{layer}", [P, CH]),
                        "rec": sb_(c2, nc, f"rec_{layer}", [P, CH]), "ob": two("ob", [P, CH]),
                        "ones": ones, "sel": sel}
                attention_stage(nc, f"att{layer}", psum, bufs, qk_d, v_d, att_d)

        with ExitStack() as c1:
            x_sb = sb_(c1, nc, "x_sb", [P, CT, T])
            scale, shift = sb_(c1, nc, "gn_scale", [P, B * CT]), sb_(c1, nc, "gn_shift", [P, B * CT])
            wq = sb_(c1, nc, "wq0", [P, CT, 3 * C])
            bv = sb_(c1, nc, "bv0", [P, C])
            group_norm_stage(nc, x_sb, scale, shift, par, gmat, x, [(const_sb[:, :], consts), (par_sb[:, :], params)])
            psum = c1.enter_context(nc.psum_tensor("psum_0", [P, 8, 512], F32))
            w = weights(qkv_w)
            qkv_stage(nc, "l0", psum, chunk_bufs(c1, "l0", False, True),
                      [(wq[:, :, 0:2 * C], w[:, :, 0:2 * C]), (wq[:, :, 2 * C:3 * C], w[:, :, 2 * C:3 * C]),
                       (bv[:, :], qkv_bv.partition_broadcast(P))],
                      {"w": wq[:, :, 0:2 * C], "w_at": 0, "wv": wq[:, :, 2 * C:3 * C], "wv_at": 1,
                       "bias": par["qkv_b"], "bv": bv, "bv_at": 2, "emb": None, "qk": qk_d, "v": v_d},
                      norm={"x": x_sb, "scale": scale, "shift": shift})
        attention(0)
        with ExitStack() as c1:
            wo = sb_(c1, nc, "wo0", [P, CT, C])
            wq = sb_(c1, nc, "wq1", [P, CT, 2 * C])
            wv = sb_(c1, nc, "wv1", [P, CT, C])
            we = sb_(c1, nc, "we1", [P, 2 * C])
            em = sb_(c1, nc, "em1", [P, 2 * SIDE])
            bufs = chunk_bufs(c1, "l1", True, True)
            bufs["emb_parts"] = sb_(c1, nc, "emb_parts", [P, 2 * CT, 2 * SIDE])
            bufs["emb_table"] = sb_(c1, nc, "emb_table", [P, 2 * CT, HW])
            bufs["sum"] = [sb_(c1, nc, f"qk_sum{n}", [P, CH]) for n in range(2)]
            psum = c1.enter_context(nc.psum_tensor("psum_1", [P, 8, 512], F32))
            qkv_stage(nc, "l1", psum, bufs,
                      [(we[:, :], w1e), (em[:, :], emb), (wo[:, :, :], weights(proj_w)),
                       (wq[:, :, :], weights(w1)), (wv[:, :, :], weights(w1v))],
                      {"w": wq, "w_at": 3, "wv": wv, "wv_at": 4, "bias": None, "bv": None,
                       "emb": {"w": we, "w_at": 0, "x": em, "x_at": 1}, "qk": qk_d, "v": v_d},
                      out_proj={"w": wo, "w_at": 2, "loads_at": 3, "bias": par["proj_b"], "att": att_d, "res": x,
                                "dst": h_d})
        attention(1)
        with ExitStack() as c1:
            wo = sb_(c1, nc, "wo1", [P, CT, C])
            psum = c1.enter_context(nc.psum_tensor("psum_2", [P, 8, 512], F32))
            output_stage(nc, "l2", psum, chunk_bufs(c1, "l2", True, False), wo, weights(wout), par["bout"], att_d,
                         h_d, out)


def position_embedding(np):
    f = np.float32
    n, side = 16, SIDE
    lx = np.log2(np.maximum(np.arange(side * n), 1).astype(f))
    lx[0] = -2.0
    lx = lx.reshape(side, n).T * np.arange(1, n + 1, dtype=f)[:, None]
    freq = np.stack([np.cos(lx), np.sin(lx)], 1).reshape(2 * n, side)
    xx = np.arange(0, n * side, dtype=f).reshape(side, n).T
    th = (np.arange(n, dtype=f) + f(0.5))[:, None] * xx / f(side * n) * f(6.283185307179586)
    time = np.stack([np.cos(th), np.sin(th)], 1).reshape(2 * n, side)
    e = np.zeros((P, 2 * side), f)
    e[0:2 * n, 0:side] = freq
    e[2 * n:4 * n, side:] = time
    return e


def constants(np):
    f = np.float32
    sel = np.zeros((P, P), f)
    for e in range(2):
        sel[64 * e, 64 * e:64 * e + 64] = 1
        sel[64 * e + 32, 64 * e:64 * e + 64] = 1
    g = np.kron(np.eye(P // GROUP, dtype=f), np.full((GROUP, GROUP), 1.0 / GROUP, f))
    return np.ascontiguousarray(np.concatenate([np.ones((P, 32), f), sel, g], 1))


def kernel(x, L0_conv_gn_w, L0_conv_gn_b, L0_conv_qkv_w, L0_conv_qkv_b, L0_conv_proj_w, L0_conv_proj_b,
           L1_conv_Wq, L1_conv_Wk, L1_conv_Wv, L1_conv_Wout, L1_conv_bout):
    import numpy as np
    import concourse.bacc as bacc
    from concourse.bass_utils import run_bass_kernel_spmd

    def cols(v):
        return np.asarray(v).reshape(-1, P).T

    qkv_w = np.asarray(L0_conv_qkv_w).reshape(8, D, 3, C).transpose(3, 2, 0, 1).reshape(C, 3 * C)
    qkv_b = np.asarray(L0_conv_qkv_b).reshape(8, D, 3).transpose(2, 0, 1).reshape(3 * C)
    wqk = np.concatenate([np.asarray(L1_conv_Wq), np.asarray(L1_conv_Wk)], 1)
    we = np.zeros((P, 2 * C), np.float32)
    we[0:D] = wqk[C:C + D]
    arrays = {
        "x": np.asarray(x).transpose(1, 0, 2, 3).reshape(C, T),
        "params": np.concatenate([cols(L0_conv_gn_w), cols(L0_conv_gn_b), cols(qkv_b[0:2 * C]),
                                  cols(L0_conv_proj_b), cols(L1_conv_bout)], 1),
        "qkv_w": qkv_w,
        "qkv_bv": qkv_b[2 * C:3 * C],
        "proj_w": np.asarray(L0_conv_proj_w).T,
        "w1": wqk[0:C], "w1v": np.asarray(L1_conv_Wv), "w1e": we,
        "wout": np.asarray(L1_conv_Wout),
        "emb": position_embedding(np),
        "consts": constants(np),
    }
    nc = bacc.Bacc("TRN2", target_bir_lowering=False, num_devices=1)
    arrays = {f"in_{k}": np.ascontiguousarray(v) for k, v in arrays.items()}
    ins = {k[3:]: nc.dram_tensor(k, v.shape, F32, kind="ExternalInput").ap() for k, v in arrays.items()}
    out = nc.dram_tensor("out_y", (C, T), F32, kind="ExternalOutput").ap()
    program(nc, **ins, out=out)
    r = run_bass_kernel_spmd(nc, [arrays], core_ids=[0])
    y = np.asarray(r.results[0]["out_y"])
    return np.ascontiguousarray(y.reshape(C, B, 48, 48).transpose(1, 0, 2, 3))
```

```python
from contextlib import ExitStack

import concourse.bass as bass
from concourse import mybir

F32 = mybir.dt.float32
F32R = mybir.dt.float32r
ALU = mybir.AluOpType
ACT = mybir.ActivationFunctionType

P = 128
SIDE = 48
B, C, HW = 2, 512, SIDE * SIDE
T = B * HW
CT = C // P
D = 64
PAIRS = C // (2 * D)
GROUP = C // 32
CH = 384
NCH = T // CH
TT = CH // P
KT = HW // P
JB = HW // CH
KC = KT // 3
SLOTS = 2 * KC
NB = B * PAIRS * JB
SCALE = float(D) ** -0.5
GN_EPS = 1e-5
NORM_STEPS = 10
SHIFT_DVE = 208
EXP_LAG = 8
PV_LAG = SLOTS + 5

PV_COUNTS = [2, 2, 2, 2, 1, 2, 1, 1, 2, 1, 1, 1]
PV_TILES = [list(range(sum(PV_COUNTS[:v]), sum(PV_COUNTS[:v + 1]))) for v in range(SLOTS)]
DEN_AT = SLOTS - KT // 2
SPREAD_AT = 1
LAST_USE = [max(max(v for v in range(SLOTS) if set(PV_TILES[v]) & {3 * c, 3 * c + 1, 3 * c + 2}),
                DEN_AT + (3 * c + 2) // 2) for c in range(KC)]

INVERT_AT = (0, 1, 2, 4, 5, 6)
PARTS = len(INVERT_AT)


def is_block(t, *numbers):
    return isinstance(t, int) and t in numbers


def sb_(ctx, nc, name, shape, dt=F32):
    return ctx.enter_context(nc.sbuf_tensor(name, shape, dt))


def norm_buffers(ctx, nc, psum, x_sb, par, gmat):
    N = B * CT
    gn = {"x": x_sb, "par": par, "gmat": gmat, "mean": psum[:, 6, 0:N], "pvar": psum[:, 7, 0:N],
          "stats": sb_(ctx, nc, "gn_stats", [P, N, JB, 6]), "mv": sb_(ctx, nc, "gn_mv", [P, N, 2])}
    for name in ("dif", "var", "sd", "rstd", "tmp", "scale", "shift"):
        gn[name] = sb_(ctx, nc, f"gn_{name}", [P, N])
    for name in ("parts_done", "tiles_done", "mean_mm", "dev_done", "var_mm", "var_done", "root_done", "step"):
        gn[name + "_sem"] = ctx.enter_context(nc.semaphore(name))
    gn["x_in"] = [ctx.enter_context(nc.semaphore(f"x_in{n}")) for n in range(N)]
    return gn


def norm_part(nc, dve, gn, n, j):
    b, c = divmod(n, CT)
    if j == 0:
        dve.wait_ge(gn["x_in"][n], 16)
    nc.vector.bn_stats(gn["stats"][:, n, j, :], gn["x"][:, c, b * HW + j * CH:b * HW + (j + 1) * CH])\
        .then_inc(gn["parts_done_sem"], 1)


def norm_tiles(nc, dve, gn, b):
    dve.wait_ge(gn["parts_done_sem"], CT * JB * (b + 1))
    for n in range(b * CT, (b + 1) * CT):
        nc.vector.bn_aggr(gn["mv"][:, n, :], gn["stats"][:, n, :, :]).then_inc(gn["tiles_done_sem"], 1)


def norm_mean(nc, pe, gn, b):
    s = slice(b * CT, (b + 1) * CT)
    pe.wait_ge(gn["tiles_done_sem"], CT * (b + 1))
    nc.tensor.matmul(gn["mean"][:, s], gn["gmat"], gn["mv"][:, s, 0], start=True, stop=True)\
        .then_inc(gn["mean_mm_sem"], 1)


def norm_variance(nc, pe, gn, b):
    s = slice(b * CT, (b + 1) * CT)
    pe.wait_ge(gn["dev_done_sem"], b + 1)
    nc.tensor.matmul(gn["pvar"][:, s], gn["gmat"], gn["var"][:, s], start=True, stop=True)\
        .then_inc(gn["var_mm_sem"], 1)


def norm_root(nc, act, gn, b):
    s = slice(b * CT, (b + 1) * CT)
    act.wait_ge(gn["var_done_sem"], b + 1)
    nc.scalar.activation(gn["sd"][:, s], gn["var"][:, s], ACT.Sqrt).then_inc(gn["root_done_sem"], 1)


def norm_scale(nc, dve, gn, b):
    s = slice(b * CT, (b + 1) * CT)
    dif, var, sd, rs, tmp = [gn[k][:, s] for k in ("dif", "var", "sd", "rstd", "tmp")]
    mean, pvar, scale, shift = [gn[k][:, s] for k in ("mean", "pvar", "scale", "shift")]
    step = gn["step_sem"]
    done = [b * NORM_STEPS]

    def in_turn(ins):
        done[0] += 1
        ins.then_inc(step, 1)
        dve.wait_ge(step, done[0])

    dve.wait_ge(gn["tiles_done_sem"], CT * (b + 1))
    dve.wait_ge(gn["mean_mm_sem"], b + 1)
    in_turn(nc.vector.tensor_tensor(dif, gn["mv"][:, s, 0], mean, ALU.subtract))
    in_turn(nc.vector.tensor_tensor(tmp, dif, dif, ALU.mult))
    nc.vector.tensor_tensor(var, tmp, gn["mv"][:, s, 1], ALU.add).then_inc(gn["dev_done_sem"], 1)
    dve.wait_ge(gn["var_mm_sem"], b + 1)
    nc.vector.tensor_scalar(var, pvar, GN_EPS, None, ALU.add).then_inc(gn["var_done_sem"], 1)
    dve.wait_ge(gn["root_done_sem"], b + 1)
    dve.wait_ge(gn["var_done_sem"], b + 1)
    in_turn(nc.vector.reciprocal(rs, sd))
    in_turn(nc.vector.tensor_tensor(tmp, rs, rs, ALU.mult))
    in_turn(nc.vector.tensor_tensor(tmp, tmp, var, ALU.mult))
    in_turn(nc.vector.tensor_scalar(tmp, tmp, -0.5, 1.5, ALU.mult, ALU.add))
    in_turn(nc.vector.tensor_tensor(rs, rs, tmp, ALU.mult))
    in_turn(nc.vector.tensor_tensor(scale, rs, gn["par"]["gn_w"], ALU.mult))
    in_turn(nc.vector.tensor_tensor(tmp, scale, mean, ALU.mult))
    in_turn(nc.vector.tensor_tensor(shift, gn["par"]["gn_b"], tmp, ALU.subtract))
    assert done[0] == (b + 1) * NORM_STEPS


def first_norm_stage(nc, gn, x_d, small, weights, w_in):
    with ExitStack() as ctx:
        small_in = ctx.enter_context(nc.semaphore("small_in"))
        block = ctx.enter_context(nc.Block())

        @block.sync
        def _(sp):
            def load_x(n):
                b, c = divmod(n, CT)
                sp.dma_start(gn["x"][:, c, b * HW:(b + 1) * HW],
                             x_d[c * P:(c + 1) * P, b * HW:(b + 1) * HW]).then_inc(gn["x_in"][n], 16)

            for n in range(CT):
                load_x(n)
                if n == 0:
                    for dst, src in small:
                        sp.dma_start(dst, src).then_inc(small_in, 16)
            for n, (dst, src) in enumerate(weights):
                sp.dma_start(dst, src).then_inc(w_in[n], 16)
            for n in range(CT, B * CT):
                load_x(n)

        @block.tensor
        def _(pe):
            pe.wait_ge(small_in, 16 * len(small))
            norm_mean(nc, pe, gn, 0)
            norm_variance(nc, pe, gn, 0)

        @block.scalar
        def _(act):
            norm_root(nc, act, gn, 0)

        @block.vector
        def _(dve):
            for n in range(CT):
                for j in range(JB):
                    norm_part(nc, dve, gn, n, j)
            norm_tiles(nc, dve, gn, 0)
            norm_scale(nc, dve, gn, 0)


def out_projection(nc, bank, w, att):
    for c in range(CT):
        mm = nc.tensor.matmul(bank, w[c], att[:, c, :], start=(c == 0), stop=(c == CT - 1))
    return mm


def qkv_stage(nc, name, psum, bufs, weights, w_in, qkv, norm=None, out_proj=None):
    with ExitStack() as ctx:
        def sem(n):
            return ctx.enter_context(nc.semaphore(f"{name}_{n}"))

        xc, att, res, hl, vo = bufs["xc"], bufs["att"], bufs["res"], bufs["hl"], bufs["vo"]
        emb, bias, bv = qkv["emb"], qkv["bias"], qkv["bv"]
        if out_proj:
            att_in = [out_proj["early"]["att_in"], sem("att_in1")]
            res_in = [out_proj["early"]["res_in"], sem("res_in1")]
        xc_ready = sem("xc_ready")
        out_mm = sem("out_mm")
        qk_mm = sem("qk_mm")
        v_mm = sem("v_mm")
        summed = sem("summed")
        high_done = sem("high_done")
        low_done = sem("low_done")
        v_done = sem("v_done")
        q_stored, k_stored = sem("q_stored"), sem("k_stored")
        v_stored = [sem(f"v_stored{p}") for p in range(2)]
        x_stored = [sem(f"x_stored{p}") for p in range(2)]
        emb_mm, emb_copied = sem("emb_mm"), sem("emb_copied")
        emb_dve, emb_pool = sem("emb_dve"), sem("emb_pool")
        block = ctx.enter_context(nc.Block())
        MT = 2 * CT

        def qk_bank(m):
            return psum[:, m % 4, 0:CH]

        def v_bank(p, tt):
            return psum[:, 4 + (TT * p + tt) % 2, 0:C]

        def out_bank(m):
            return psum[:, 6 + m % 2, 0:CH]

        def tokens(i):
            return bass.ds(i * CH, CH)

        def pairs_of_chunks(engine, pair):
            pair(0, False)
            with engine.Fori(1, NCH // 2 - 1) as it:
                pair(it, False)
            pair(NCH // 2 - 1, True)

        def add_embedding(engine, m):
            rows = bufs["emb_parts"][:, m, 0:SIDE].unsqueeze(2).broadcast_to([P, SIDE, SIDE])
            cols = bufs["emb_parts"][:, m, SIDE:2 * SIDE].unsqueeze(1).broadcast_to([P, SIDE, SIDE])
            return engine.tensor_tensor(bufs["emb_table"][:, m, :].rearrange("p (h w) -> p h w", h=SIDE),
                                        rows, cols, ALU.add)

        @block.sync
        def _(sp):
            def load_att(i, p):
                sp.dma_start(att[p][:, :, :], out_proj["att"].rearrange("(c p) t -> p c t", p=P)[:, :, tokens(i)])\
                    .then_inc(att_in[p], 16)

            def load_res(i, p):
                sp.dma_start(res[p][:, :, :], out_proj["res"].rearrange("(c p) t -> p c t", p=P)[:, :, tokens(i)])\
                    .then_inc(res_in[p], 16)

            for dst, src, signal in weights:
                sp.dma_start(dst, src).then_inc(signal, 16)
            if out_proj:
                load_att(1, 1)
                load_res(1, 1)

            def pair(it, last):
                for p in range(2):
                    i = 2 * it + p
                    if out_proj:
                        if not last:
                            sp.wait_ge(out_mm, CT * (i + 1))
                            load_att(i + 2, p)
                        sp.wait_ge(xc_ready, CT * (i + 1))
                        if not last:
                            load_res(i + 2, p)
                        sp.dma_start(out_proj["dst"].rearrange("(c p) t -> p c t", p=P)[:, :, tokens(i)],
                                     xc[p][:, :, :]).then_inc(x_stored[p], 16)
                    for half, stored in ((0, q_stored), (1, k_stored)):
                        sp.wait_ge(low_done, MT * i + CT * (half + 1))
                        sp.dma_start(qkv["qk"].rearrange("m w p t -> p (m w) t")[:, half * MT:(half + 1) * MT, tokens(i)],
                                     hl[half].rearrange("p m w t -> p (m w) t")).then_inc(stored, 16)
                    sp.wait_ge(v_done, TT * (i + 1))
                    sp.dma_start(qkv["v"][tokens(i), :].rearrange("(a p) d -> p a d", p=P),
                                 vo[p][:, :, :]).then_inc(v_stored[p], 16)

            pairs_of_chunks(sp, pair)
            for p in range(2):
                if out_proj:
                    sp.wait_ge(x_stored[p], 16 * (NCH // 2))
                sp.wait_ge(v_stored[p], 16 * (NCH // 2))
            sp.wait_ge(q_stored, 16 * NCH)
            sp.wait_ge(k_stored, 16 * NCH)

        @block.tensor
        def _(pe):
            def out_tiles(i, p):
                pe.wait_ge(att_in[p], 16 * (i // 2 + 1))
                for m in range(CT):
                    if m >= 2:
                        pe.wait_ge(xc_ready, CT * i + m - 1)
                    elif m == 0 and not is_block(i, 0):
                        pe.wait_ge(xc_ready, CT * i)
                    w = [out_proj["w"][:, c, m * P:(m + 1) * P] for c in range(CT)]
                    out_projection(nc, out_bank(m), w, att[p]).then_inc(out_mm, 1)

            if emb:
                pe.wait_ge(w_in[emb["w_at"]], 16)
                pe.wait_ge(w_in[emb["x_at"]], 16)
                for m in range(MT):
                    mm = nc.tensor.matmul(psum[:, 4 + m // 4, (m % 4) * P:(m % 4) * P + 2 * SIDE],
                                          emb["w"][:, m * P:(m + 1) * P], emb["x"][:, :], start=True, stop=True)
                mm.then_inc(emb_mm, 1)
            if out_proj:
                pe.wait_ge(w_in[out_proj["w_at"]], 16)
                out_tiles(0, 0)
            pe.wait_ge(w_in[qkv["w_at"]], 16)

            def pair(it, last):
                for p in range(2):
                    i = 2 * it + p
                    pe.wait_ge(xc_ready, CT * (i + 1))
                    for m in range(MT):
                        if m >= 4:
                            pe.wait_ge(low_done, MT * i + m - 3)
                        elif m == 0 and not is_block(i, 0):
                            pe.wait_ge(low_done, MT * i)
                        for c in range(CT):
                            mm = nc.tensor.matmul(qk_bank(m), qkv["w"][:, c, m * P:(m + 1) * P], xc[p][:, c, :],
                                                  start=(c == 0), stop=(c == CT - 1))
                        mm.then_inc(qk_mm, 1)
                    if norm and is_block(i, 1):
                        norm_mean(nc, pe, norm, 1)
                    if out_proj and not (last and p == 1):
                        out_tiles(i + 1, 1 - p)
                    if is_block(i, 0):
                        pe.wait_ge(w_in[qkv["wv_at"]], 16)
                        if emb:
                            pe.wait_ge(emb_copied, 1)
                    for tt in range(TT):
                        if tt >= 2:
                            pe.wait_ge(v_done, TT * i + tt - 1)
                        elif tt == 0 and not is_block(i, 0):
                            pe.wait_ge(v_done, TT * i)
                        for c in range(CT):
                            mm = nc.tensor.matmul(v_bank(p, tt), xc[p][:, c, tt * P:(tt + 1) * P], qkv["wv"][:, c, :],
                                                  start=(c == 0), stop=(c == CT - 1))
                        mm.then_inc(v_mm, 1)
                        if norm and is_block(i, 1) and tt == 0:
                            norm_variance(nc, pe, norm, 1)

            pairs_of_chunks(pe, pair)

        @block.scalar
        def _(act):
            if emb:
                act.wait_ge(emb_mm, 1)
                nc.scalar.activation(bufs["emb_parts"][:, :, :].rearrange("p (a m) t -> p a m t", a=2),
                                     psum[:, 4:6, :].rearrange("p a (m t) -> p a m t", m=4)[:, :, :, 0:2 * SIDE],
                                     ACT.Copy).then_inc(emb_copied, 1)

            def pair(it, last):
                for p in range(2):
                    i = 2 * it + p
                    for m in range(MT):
                        half, mt = divmod(m, CT)
                        if mt == 0 and not is_block(i, 0):
                            act.wait_ge((q_stored, k_stored)[half], 16 * i)
                        high = hl[half][:, mt, 0, :].bitcast(F32R)
                        if emb:
                            act.wait_ge(summed, MT * i + m + 1)
                            a = nc.scalar.activation(high, bufs["sum"][m % 2][:, :], ACT.Copy)
                        else:
                            act.wait_ge(qk_mm, MT * i + m + 1)
                            a = nc.scalar.activation(high, qk_bank(m), ACT.Identity, bias=bias[:, m:m + 1])
                        a.then_inc(high_done, 1)
                    if norm and is_block(i, 1):
                        norm_root(nc, act, norm, 1)

            pairs_of_chunks(act, pair)

        @block.gpsimd
        def _(pool):
            if emb:
                pool.wait_ge(emb_copied, 1)
                for m in range(1, MT, 2):
                    add_embedding(nc.gpsimd, m).then_inc(emb_pool, 1)

        @block.vector
        def _(dve):
            def input_chunk(i, p):
                if out_proj:
                    dve.wait_ge(res_in[p], 16 * (i // 2 + 1))
                if not is_block(i, 0, 1):
                    if out_proj:
                        dve.wait_ge(x_stored[p], 16 * (i // 2))
                    dve.wait_ge(v_mm, TT * (i - 1))
                for c in range(CT):
                    if out_proj:
                        dve.wait_ge(out_mm, CT * i + c + 1)
                        d = nc.vector.scalar_tensor_tensor(out=xc[p][:, c, :], in0=out_bank(c),
                                                           scalar=out_proj["bias"][:, c:c + 1], in1=res[p][:, c, :],
                                                           op0=ALU.add, op1=ALU.add)
                    else:
                        n = bass.ds(i // JB * CT + c, 1)
                        d = nc.vector.tensor_scalar(xc[p][:, c, :], norm["x"][:, c, tokens(i)], norm["scale"][:, n],
                                                    norm["shift"][:, n], ALU.mult, ALU.add)
                    d.then_inc(xc_ready, 1)

            if emb:
                dve.wait_ge(emb_copied, 1)
                for m in range(0, MT, 2):
                    if m == 2:
                        input_chunk(0, 0)
                    add_embedding(nc.vector, m).then_inc(emb_dve, 1)
            else:
                input_chunk(0, 0)

            def pair(it, last):
                for p in range(2):
                    i = 2 * it + p
                    for m in range(MT):
                        half, mt = divmod(m, CT)
                        high, low = hl[half][:, mt, 0, :], hl[half][:, mt, 1, :].bitcast(F32R)
                        if emb:
                            if is_block(i, 0):
                                dve.wait_ge((emb_dve, emb_pool)[m % 2], m // 2 + 1)
                            dve.wait_ge(qk_mm, MT * i + m + 1)
                            if not (is_block(i, 0) and m < 2):
                                dve.wait_ge(low_done, MT * i + m - 1)
                            nc.vector.tensor_tensor(bufs["sum"][m % 2][:, :], qk_bank(m),
                                                    emb_of(i, m), ALU.add).then_inc(summed, 1)
                            dve.wait_ge(high_done, MT * i + m + 1)
                            nc.vector.tensor_tensor(low, bufs["sum"][m % 2][:, :], high, ALU.subtract)\
                                .then_inc(low_done, 1)
                        else:
                            dve.wait_ge(high_done, MT * i + m + 1)
                            nc.vector.scalar_tensor_tensor(out=low, in0=qk_bank(m), scalar=bias[:, m:m + 1], in1=high,
                                                           op0=ALU.add, op1=ALU.subtract).then_inc(low_done, 1)
                        if norm and is_block(i, 1):
                            for k in range(m * CT * JB // MT, (m + 1) * CT * JB // MT):
                                norm_part(nc, dve, norm, CT + k // JB, k % JB)
                    if norm and is_block(i, 1):
                        norm_tiles(nc, dve, norm, 1)
                    if not (last and p == 1):
                        input_chunk(i + 1, 1 - p)
                    if norm and is_block(i, 1):
                        norm_scale(nc, dve, norm, 1)
                    for tt in range(TT):
                        if tt == 0 and not is_block(i, 0, 1):
                            dve.wait_ge(v_stored[p], 16 * it)
                        dve.wait_ge(v_mm, TT * i + tt + 1)
                        if bv is not None and is_block(i, 0):
                            dve.wait_ge(w_in[qkv["bv_at"]], 16)
                        if bv is not None:
                            d = nc.vector.tensor_tensor(vo[p][:, tt, :], v_bank(p, tt), bv[:, :], ALU.add)
                        else:
                            d = nc.vector.tensor_copy(vo[p][:, tt, :], v_bank(p, tt))
                        d.then_inc(v_done, 1)

            def emb_of(i, m):
                return bufs["emb_table"][:, m, bass.ds(i % JB * CH, CH)]

            pairs_of_chunks(dve, pair)


def output_stage(nc, name, psum, bufs, early, bias, att_d, res_d, out_d):
    with ExitStack() as ctx:
        def sem(n):
            return ctx.enter_context(nc.semaphore(f"{name}_{n}"))

        xc, att, res = bufs["xc"], bufs["att"], bufs["res"]
        w, w_in = early["w"], early["w_in"]
        att_in = [early["att_in"], sem("att_in1")]
        res_in = [early["res_in"], sem("res_in1")]
        out_mm, summed = sem("out_mm"), sem("summed")
        stored = [sem(f"stored{p}") for p in range(2)]
        block = ctx.enter_context(nc.Block())

        def rows(d, i):
            return d.rearrange("(c p) t -> p c t", p=P)[:, :, bass.ds(i * CH, CH)]

        def bank(p, m):
            return psum[:, CT * p + m, 0:CH]

        @block.sync
        def _(sp):
            sp.dma_start(att[1][:, :, :], rows(att_d, 1)).then_inc(att_in[1], 16)
            sp.dma_start(res[1][:, :, :], rows(res_d, 1)).then_inc(res_in[1], 16)
            with sp.Fori(0, NCH // 2 - 1) as it:
                for p in range(2):
                    i = 2 * it + p
                    sp.wait_ge(out_mm, CT * (i + 1))
                    sp.dma_start(att[p][:, :, :], rows(att_d, i + 2)).then_inc(att_in[p], 16)
                    sp.wait_ge(summed, CT * (i + 1))
                    sp.dma_start(res[p][:, :, :], rows(res_d, i + 2)).then_inc(res_in[p], 16)

        @block.scalar
        def _(act):
            with act.Fori(0, NCH // 2) as it:
                for p in range(2):
                    act.wait_ge(summed, CT * (2 * it + p + 1))
                    act.dma_start(rows(out_d, 2 * it + p), xc[p][:, :, :]).then_inc(stored[p], 16)
            for p in range(2):
                act.wait_ge(stored[p], 16 * (NCH // 2))

        @block.tensor
        def _(pe):
            pe.wait_ge(w_in, 16)

            def pair(it):
                for p in range(2):
                    i = 2 * it + p
                    pe.wait_ge(att_in[p], 16 * (it + 1))
                    if not is_block(i, 0, 1):
                        pe.wait_ge(summed, CT * (i - 1))
                    for m in range(CT):
                        out_projection(nc, bank(p, m), [w[:, c, m * P:(m + 1) * P] for c in range(CT)], att[p])\
                            .then_inc(out_mm, 1)

            pair(0)
            with pe.Fori(1, NCH // 2) as it:
                pair(it)

        @block.vector
        def _(dve):
            def pair(it):
                for p in range(2):
                    i = 2 * it + p
                    dve.wait_ge(res_in[p], 16 * (it + 1))
                    if not is_block(i, 0, 1):
                        dve.wait_ge(stored[p], 16 * it)
                    for m in range(CT):
                        dve.wait_ge(out_mm, CT * i + m + 1)
                        nc.vector.scalar_tensor_tensor(out=xc[p][:, m, :], in0=bank(p, m), scalar=bias[:, m:m + 1],
                                                       in1=res[p][:, m, :], op0=ALU.add, op1=ALU.add)\
                            .then_inc(summed, 1)

            pair(0)
            with dve.Fori(1, NCH // 2) as it:
                pair(it)


def attention_stage(nc, name, psum, bufs, qk_d, v_d, att_d, next_loads):
    with ExitStack() as ctx:
        def sem(n):
            return ctx.enter_context(nc.semaphore(f"{name}_{n}"))

        kst, qst, vst, prob = bufs["kst"], bufs["qst"], bufs["vst"], bufs["prob"]
        run, fold, mx = bufs["run"], bufs["fold"], bufs["mx"]
        den, dsp, pvr, rec, ob = bufs["den"], bufs["dsp"], bufs["pvr"], bufs["rec"], bufs["ob"]
        ones, sel = bufs["ones"], bufs["sel"]
        q_in = [sem(f"q_in{p}") for p in range(2)]
        k_in = [sem(f"k_in{c}") for c in range(KC)]
        v_in = [sem(f"v_in{c}") for c in range(KC)]
        scored = sem("scored")
        copied = sem("copied")
        maxed = sem("maxed")
        folded = sem("folded")
        reducing = sem("reducing")
        mx_ready = sem("mx_ready")
        dve_shifted, pool_shifted = sem("dve_shifted"), sem("pool_shifted")
        exp_done = sem("exp_done")
        pv_done = sem("pv_done")
        den_copied, pv_copied = sem("den_copied"), sem("pv_copied")
        spread = sem("spread")
        spread_copied = sem("spread_copied")
        inverted = sem("inverted")
        normed = sem("normed")
        stored = [sem(f"stored{p}") for p in range(2)]
        block = ctx.enter_context(nc.Block())

        def scored_count(g):
            return SLOTS + g + 1

        def pv_count(t, v):
            return 2 * SLOTS + SLOTS * t + v + 1

        def shifted_count(g):
            return SLOTS + g + 1

        def maxed_count(t, s):
            return (SLOTS - 2) * t + s - s // KC

        def normed_count(t):
            return t + 2

        def s_bank(g):
            return psum[:, 3 * (g % 2):3 * (g % 2) + 3, 0:CH]

        pv_bank = psum[:, 6, 0:CH]
        den_bank = psum[:, 7, 0:CH]

        def chunk_of(par, s):
            e, c = divmod(s, KC)
            return prob[par][:, e, 3 * c:3 * c + 3, :]

        def parity(par, s):
            return (par + s // SLOTS) % 2, s % SLOTS

        def shift_part(engine, x, e, q0, q1):
            return engine.tensor_tensor(x[:, :, q0:q1], x[:, :, q0:q1],
                                        mx[e][:, q0:q1].unsqueeze(1).broadcast_to([P, 3, q1 - q0]), ALU.subtract)

        @block.sync
        def _(sp):
            with sp.Fori(0, B) as b, sp.Fori(0, PAIRS) as hp:
                pair = b * PAIRS + hp
                for j in range(JB):
                    t = pair * JB + j
                    sp.wait_ge(scored, scored_count(SLOTS * t - SLOTS - 1))
                    for half in range(2):
                        sp.dma_start(
                            qst[j % 2][half * D:(half + 1) * D, :, :].bitcast(F32),
                            qk_d[bass.ds(hp, 1), :, :, bass.ds(b * HW + j * CH, CH)]
                            .rearrange("m w (e p) t -> p (m w e) t", e=2)).then_inc(q_in[j % 2], 16)
                    if j == 0:
                        for c in range(KC):
                            sp.wait_ge(scored, scored_count(SLOTS * (t - 1) + KC + c))
                            for w in range(2):
                                sp.dma_start(
                                    kst[w * D:(w + 1) * D, :, c * CH:(c + 1) * CH].bitcast(F32),
                                    qk_d[bass.ds(PAIRS + hp, 1), w, :, bass.ds(b * HW + c * CH, CH)]
                                    .rearrange("m (e p) t -> p (m e) t", e=2)).then_inc(k_in[c], 16)
                    if j == 1:
                        for c in range(KC):
                            sp.wait_ge(pv_done, pv_count(t - 2, LAST_USE[c]))
                            sp.dma_start(
                                vst[:, 3 * c:3 * c + 3, :],
                                v_d[bass.ds(b * HW + c * CH, CH), bass.ds(hp * P, P)]
                                .rearrange("(a p) d -> p a d", p=P)).then_inc(v_in[c], 16)
            for p in range(2):
                sp.wait_ge(stored[p], 16 * (NB // (2 * B)))
            for dst, src, signal in next_loads:
                sp.dma_start(dst, src).then_inc(signal, 16)

        @block.tensor
        def _(pe):
            pe.sem_inc(scored, SLOTS)
            pe.sem_inc(pv_done, 2 * SLOTS)

            def scores(t, par, s):
                bp, bs = parity(par, s)
                blk = t + s // SLOTS
                g = SLOTS * t + s
                e, c = divmod(bs, KC)
                if bs == 0:
                    pe.wait_ge(q_in[bp], 32 * (blk // 2 + 1))
                if e == 0:
                    pe.wait_ge(k_in[c], 32 * (blk // JB + 1))
                if not (is_block(t, 0) and s < 2):
                    pe.wait_ge(copied, g - 1)
                for k in range(3):
                    for w in range(2):
                        mm = nc.tensor.matmul(psum[:, 3 * (s % 2) + k, 0:CH],
                                              kst[:, e, (3 * c + k) * P:(3 * c + k + 1) * P],
                                              qst[bp][:, 2 * w + e, :], start=(w == 0), stop=(w == 1))
                mm.then_inc(scored, 1)

            def spread_den(t):
                pe.wait_ge(den_copied, t + 1)
                nc.tensor.matmul(den_bank, sel[:, :], den[:, :], start=True, stop=True).then_inc(spread, 1)

            def weigh(t, par, v):
                if v == 0:
                    pe.wait_ge(pv_copied, t)
                for kt in PV_TILES[v]:
                    if kt % 3 == 0:
                        pe.wait_ge(v_in[kt // 3], 16 * (t // JB + 1))
                        pe.wait_ge(exp_done, SLOTS * t + KC + kt // 3 + 1)
                    for e in range(2):
                        mm = nc.tensor.matmul(psum[e * D:(e + 1) * D, 6, 0:CH], vst[:, kt, e * D:(e + 1) * D],
                                              prob[par][:, e, kt, :], start=(kt == 0), stop=(kt == KT - 1))
                if v >= DEN_AT:
                    j = v - DEN_AT
                    if j == 0:
                        pe.wait_ge(spread_copied, t)
                    for e in range(2):
                        for odd in range(2):
                            r = 64 * e + 32 * odd
                            mm = nc.tensor.matmul(psum[r:r + 32, 7, 0:CH], ones[:, :],
                                                  prob[par][:, e, 2 * j + odd, :], start=(j == 0),
                                                  stop=(j == KT // 2 - 1), tile_position=(0, r))
                mm.then_inc(pv_done, 1)

            def body(t, par, n_scores=SLOTS):
                for v in range(SLOTS):
                    if v == SPREAD_AT and not is_block(t, 0):
                        spread_den(t - 1)
                    weigh(t, par, v)
                    if v < n_scores:
                        scores(t, par, PV_LAG + v)

            for s in range(PV_LAG):
                scores(0, 0, s)
            body(0, 0)
            with pe.Fori(0, (NB - 4) // 2) as it:
                for p in range(2):
                    body(2 * it + 1 + p, 1 - p)
            for t in range(NB - 3, NB):
                body(t, t % 2, n_scores=max(0, min(SLOTS, SLOTS * (NB - t) - PV_LAG)))
            spread_den(NB - 1)

        @block.scalar
        def _(act):
            def copy(t, par, s):
                bp, bs = parity(par, s)
                blk = t + s // SLOTS
                g = SLOTS * t + s
                if bs % KC == 0:
                    act.wait_ge(scored, scored_count(g))
                else:
                    act.wait_ge(maxed, maxed_count(blk, bs))
                act.wait_ge(pv_done, pv_count(blk - 2, LAST_USE[bs % KC]))
                nc.scalar.activation(chunk_of(bp, bs), s_bank(s), ACT.Copy).then_inc(copied, 1)

            def exponential(t, par, s):
                act.wait_ge(dve_shifted, shifted_count(SLOTS * t + s))
                act.wait_ge(pool_shifted, shifted_count(SLOTS * t + s))
                x = chunk_of(par, s)
                nc.scalar.activation(x, x, ACT.Exp, scale=SCALE).then_inc(exp_done, 1)

            def evacuate(t, par):
                act.wait_ge(pv_done, pv_count(t, SLOTS - 1))
                if not is_block(t, 0):
                    act.wait_ge(normed, normed_count(t - 2))
                nc.scalar.activation(pvr[par][:, :], pv_bank, ACT.Copy).then_inc(pv_copied, 1)
                act.wait_ge(spread, t)
                nc.scalar.activation(den[:, :], den_bank, ACT.Copy).then_inc(den_copied, 1)

            def copy_spread(t):
                act.wait_ge(spread, t + 1)
                act.wait_ge(inverted, PARTS * t)
                nc.scalar.activation(dsp[:, :], den_bank, ACT.Copy).then_inc(spread_copied, 1)

            def store(t, par):
                pair = t // JB
                pair_row, j_off = (pair % PAIRS) * P, (pair // PAIRS) * HW + (t % JB) * CH
                act.wait_ge(normed, normed_count(t))
                act.dma_start(att_d[bass.ds(pair_row, P), bass.ds(j_off, CH)], ob[par][:, :])\
                    .then_inc(stored[par], 16)

            def body(t, par, n_copies=SLOTS):
                for k in range(SLOTS):
                    if k == PV_LAG - 2 - EXP_LAG and not is_block(t, 0):
                        evacuate(t - 1, 1 - par)
                    if k < n_copies:
                        copy(t, par, EXP_LAG + k)
                    if k == PV_LAG - EXP_LAG and not is_block(t, 0):
                        copy_spread(t - 1)
                    exponential(t, par, k)
                if not is_block(t, 0, 1):
                    store(t - 2, par)

            for s in range(EXP_LAG):
                copy(0, 0, s)
            for t in range(2):
                body(t, t)
            with act.Fori(0, (NB - 4) // 2) as it:
                for p in range(2):
                    body(2 * it + 2 + p, p)
            body(NB - 2, 0)
            body(NB - 1, 1, n_copies=SLOTS - EXP_LAG)
            store(NB - 2, 0)
            evacuate(NB - 1, 1)
            copy_spread(NB - 1)
            store(NB - 1, 1)
            for p in range(2):
                act.wait_ge(stored[p], 16 * (NB // 2))

        @block.gpsimd
        def _(pool):
            pool.sem_inc(pool_shifted, SLOTS)
            with pool.Fori(0, NB // 2) as it:
                for par in range(2):
                    t = 2 * it + par
                    for e in range(2):
                        u = 2 * t + e
                        pool.wait_ge(folded, 2 * (u + 1))
                        pool.wait_ge(dve_shifted, shifted_count(KC * (u - 1) - 1))
                        pool.wait_ge(pool_shifted, shifted_count(KC * (u - 1) - 1))
                        pool.sem_inc(reducing, 1)
                        nc.gpsimd.partition_all_reduce(mx[e][:, :], fold[e][:, :], P, bass.bass_isa.ReduceOp.max)\
                            .then_inc(mx_ready, 1)
                        for c in range(KC):
                            pool.wait_ge(mx_ready, u + 1)
                            pool.wait_ge(copied, SLOTS * t + KC * e + c + 1)
                            shift_part(nc.gpsimd, chunk_of(par, KC * e + c), e, SHIFT_DVE, CH)\
                                .then_inc(pool_shifted, 1)

        @block.vector
        def _(dve):
            def maximum(t, par, s, first_units=False):
                g = SLOTS * t + s
                bp, bs = parity(par, s)
                e, c = divmod(bs, KC)
                u = 2 * t + s // KC
                if c == 0:
                    return
                r = run[e]
                dve.wait_ge(scored, scored_count(g))
                before = maxed_count(t + s // SLOTS, bs) - 1
                if c == 1:
                    dve.wait_ge(copied, g)
                    if not (first_units and s < SLOTS):
                        dve.wait_ge(folded, 2 * (u - 1))
                    other = chunk_of(bp, bs - 1)
                else:
                    dve.wait_ge(maxed, before)
                    other = r[:, :, :]
                nc.vector.tensor_tensor(r[:, :, :], s_bank(s), other, ALU.max).then_inc(maxed, 1)
                if c == KC - 1:
                    dve.wait_ge(maxed, before + 1)
                    if not (first_units and s < SLOTS):
                        dve.wait_ge(mx_ready, u - 1)
                    nc.vector.tensor_tensor(fold[e][:, :], r[:, 0, :], r[:, 1, :], ALU.max).then_inc(folded, 1)
                    dve.wait_ge(folded, 2 * u + 1)
                    nc.vector.tensor_tensor(fold[e][:, :], fold[e][:, :], r[:, 2, :], ALU.max).then_inc(folded, 1)

            def shift(t, par, s):
                dve.wait_ge(mx_ready, 2 * t + s // KC + 1)
                dve.wait_ge(copied, SLOTS * t + s + 1)
                shift_part(nc.vector, chunk_of(par, s), s // KC, 0, SHIFT_DVE).then_inc(dve_shifted, 1)

            def invert(t, part):
                dve.wait_ge(spread_copied, t + 1)
                dve.wait_ge(normed, normed_count(t - 1))
                q = slice(part * CH // PARTS, (part + 1) * CH // PARTS)
                nc.vector.reciprocal(rec[:, q], dsp[:, q]).then_inc(inverted, 1)

            def norm(t, par):
                dve.wait_ge(inverted, PARTS * (t + 1))
                dve.wait_ge(pv_copied, t + 1)
                if not is_block(t, 0, 1):
                    dve.wait_ge(stored[par], 16 * (t // 2))
                nc.vector.tensor_tensor(ob[par][:, :], pvr[par][:, :], rec[:, :], ALU.mult).then_inc(normed, 1)

            def body(t, par, n_max=SLOTS):
                for k in range(SLOTS):
                    if k < n_max:
                        maximum(t, par, EXP_LAG + k, first_units=is_block(t, 0))
                    if not is_block(t, 0, 1):
                        for part in range(PARTS):
                            if INVERT_AT[part] == k:
                                invert(t - 2, part)
                        if k == INVERT_AT[-1] + 1:
                            norm(t - 2, par)
                    shift(t, par, k)

            dve.sem_inc(dve_shifted, SLOTS)
            dve.sem_inc(normed, 1)
            for s in range(EXP_LAG):
                maximum(0, 0, s, first_units=True)
            for t in range(2):
                body(t, t)
            with dve.Fori(0, (NB - 4) // 2) as it:
                for p in range(2):
                    body(2 * it + 2 + p, p)
            body(NB - 2, 0)
            body(NB - 1, 1, n_max=SLOTS - EXP_LAG)
            for t in (NB - 2, NB - 1):
                for part in range(PARTS):
                    invert(t, part)
                norm(t, t % 2)


def program(nc, x, params, qkv_w, qkv_bv, proj_w, w1, w1v, w1e, wout, emb, consts, out):
    def dram(name, shape, dt=F32):
        return nc.dram_tensor(name, shape, dt, kind="Internal").ap()

    qk_d = dram("qk_scratch", (2 * CT, 2, P, T))
    v_d = dram("v_scratch", (T, C))
    att_d = dram("att_scratch", (C, T))
    h_d = dram("h_scratch", (C, T))

    with ExitStack() as ctx:
        const_sb = sb_(ctx, nc, "const_sb", [P, 32 + P + P])
        par_sb = sb_(ctx, nc, "par_sb", [P, 2 * CT + 2 * CT + CT + CT])
        ones, sel, gmat = const_sb[:, 0:32], const_sb[:, 32:32 + P], const_sb[:, 32 + P:32 + 2 * P]
        par = {"gn_w": par_sb[:, 0:CT], "gn_b": par_sb[:, CT:2 * CT], "qkv_b": par_sb[:, 2 * CT:4 * CT],
               "proj_b": par_sb[:, 4 * CT:5 * CT], "bout": par_sb[:, 5 * CT:6 * CT]}

        def weights(w):
            return w.rearrange("(c p) n -> p c n", p=P)

        def chunk_bufs(c2, stage, early, qkv):
            def two(name, shape):
                return [sb_(c2, nc, f"{name}{i}_{stage}", shape) for i in range(2)]

            def second(name):
                return sb_(c2, nc, f"{name}1_{stage}", [P, CT, CH])

            return {"xc": two("xc", [P, CT, CH]),
                    "att": [early["att"], second("attc")] if early else None,
                    "res": [early["res"], second("resc")] if early else None,
                    "hl": two("hl", [P, CT, 2, CH]) if qkv else None,
                    "vo": two("vo", [P, TT, C]) if qkv else None}

        def rows(d, i):
            return d.rearrange("(c p) t -> p c t", p=P)[:, :, i * CH:(i + 1) * CH]

        def early_loads(c1, stage, w, res_d):
            early = {"w": sb_(c1, nc, f"wo_{stage}", [P, CT, C]), "att": sb_(c1, nc, f"attc0_{stage}", [P, CT, CH]),
                     "res": sb_(c1, nc, f"resc0_{stage}", [P, CT, CH])}
            for signal in ("w_in", "att_in", "res_in"):
                early[signal] = c1.enter_context(nc.semaphore(f"{signal}_{stage}"))
            return early, [(early["w"][:, :, :], weights(w), early["w_in"]),
                           (early["att"][:, :, :], rows(att_d, 0), early["att_in"]),
                           (early["res"][:, :, :], rows(res_d, 0), early["res_in"])]

        def attention(layer, next_loads):
            with ExitStack() as c2:
                psum = c2.enter_context(nc.psum_tensor(f"psum_att{layer}", [P, 8, 512], F32))

                def two(name, shape, dt=F32):
                    return [sb_(c2, nc, f"{name}{i}_{layer}", shape, dt) for i in range(2)]

                bufs = {"kst": sb_(c2, nc, f"kst_{layer}", [P, 2, HW], F32R), "qst": two("qst", [P, 4, CH], F32R),
                        "vst": sb_(c2, nc, f"vst_{layer}", [P, KT, P]), "prob": two("prob", [P, 2, KT, CH]),
                        "run": two("run", [P, 3, CH]), "fold": two("fold", [P, CH]), "mx": two("mx", [P, CH]),
                        "den": sb_(c2, nc, f"den_{layer}", [P, CH]), "dsp": sb_(c2, nc, f"dsp_{layer}", [P, CH]),
                        "pvr": two("pvr", [P, CH]),
                        "rec": sb_(c2, nc, f"rec_{layer}", [P, CH]), "ob": two("ob", [P, CH]),
                        "ones": ones, "sel": sel}
                attention_stage(nc, f"att{layer}", psum, bufs, qk_d, v_d, att_d, next_loads)

        def semaphores(c1, stage, n):
            return [c1.enter_context(nc.semaphore(f"w_in{i}_{stage}")) for i in range(n)]

        with ExitStack() as c1:
            x_sb = sb_(c1, nc, "x_sb", [P, CT, T])
            wq = sb_(c1, nc, "wq0", [P, CT, 3 * C])
            bv = sb_(c1, nc, "bv0", [P, C])
            psum = c1.enter_context(nc.psum_tensor("psum_0", [P, 8, 512], F32))
            gn = norm_buffers(c1, nc, psum, x_sb, par, gmat)
            w = weights(qkv_w)
            w_in = semaphores(c1, "l0", 3)
            first_norm_stage(nc, gn, x, [(const_sb[:, :], consts), (par_sb[:, :], params)],
                             [(wq[:, :, 0:2 * C], w[:, :, 0:2 * C]), (wq[:, :, 2 * C:3 * C], w[:, :, 2 * C:3 * C]),
                              (bv[:, :], qkv_bv.partition_broadcast(P))], w_in)
            qkv_stage(nc, "l0", psum, chunk_bufs(c1, "l0", None, True), [], w_in,
                      {"w": wq[:, :, 0:2 * C], "w_at": 0, "wv": wq[:, :, 2 * C:3 * C], "wv_at": 1,
                       "bias": par["qkv_b"], "bv": bv, "bv_at": 2, "emb": None, "qk": qk_d, "v": v_d}, norm=gn)
        with ExitStack() as c1:
            early, loads = early_loads(c1, "l1", proj_w, x)
            we = sb_(c1, nc, "we1", [P, 2 * C])
            em = sb_(c1, nc, "em1", [P, 2 * SIDE])
            we_in, em_in, wq_in, wv_in = semaphores(c1, "l1", 4)
            attention(0, [(we[:, :], w1e, we_in), (em[:, :], emb, em_in)] + loads)
            wq = sb_(c1, nc, "wq1", [P, CT, 2 * C])
            wv = sb_(c1, nc, "wv1", [P, CT, C])
            bufs = chunk_bufs(c1, "l1", early, True)
            bufs["emb_parts"] = sb_(c1, nc, "emb_parts", [P, 2 * CT, 2 * SIDE])
            bufs["emb_table"] = sb_(c1, nc, "emb_table", [P, 2 * CT, HW])
            bufs["sum"] = [sb_(c1, nc, f"qk_sum{n}", [P, CH]) for n in range(2)]
            psum = c1.enter_context(nc.psum_tensor("psum_1", [P, 8, 512], F32))
            qkv_stage(nc, "l1", psum, bufs,
                      [(wq[:, :, :], weights(w1), wq_in), (wv[:, :, :], weights(w1v), wv_in)],
                      [we_in, em_in, early["w_in"], wq_in, wv_in],
                      {"w": wq, "w_at": 3, "wv": wv, "wv_at": 4, "bias": None, "bv": None,
                       "emb": {"w": we, "w_at": 0, "x": em, "x_at": 1}, "qk": qk_d, "v": v_d},
                      out_proj={"w": early["w"], "w_at": 2, "bias": par["proj_b"], "att": att_d, "res": x,
                                "dst": h_d, "early": early})
        with ExitStack() as c1:
            early, loads = early_loads(c1, "l2", wout, h_d)
            attention(1, loads)
            psum = c1.enter_context(nc.psum_tensor("psum_2", [P, 8, 512], F32))
            output_stage(nc, "l2", psum, chunk_bufs(c1, "l2", early, False), early, par["bout"], att_d, h_d, out)


def position_embedding(np):
    f = np.float32
    n, side = 16, SIDE
    lx = np.log2(np.maximum(np.arange(side * n), 1).astype(f))
    lx[0] = -2.0
    lx = lx.reshape(side, n).T * np.arange(1, n + 1, dtype=f)[:, None]
    freq = np.stack([np.cos(lx), np.sin(lx)], 1).reshape(2 * n, side)
    xx = np.arange(0, n * side, dtype=f).reshape(side, n).T
    th = (np.arange(n, dtype=f) + f(0.5))[:, None] * xx / f(side * n) * f(6.283185307179586)
    time = np.stack([np.cos(th), np.sin(th)], 1).reshape(2 * n, side)
    e = np.zeros((P, 2 * side), f)
    e[0:2 * n, 0:side] = freq
    e[2 * n:4 * n, side:] = time
    return e


def constants(np):
    f = np.float32
    sel = np.zeros((P, P), f)
    for e in range(2):
        sel[64 * e, 64 * e:64 * e + 64] = 1
        sel[64 * e + 32, 64 * e:64 * e + 64] = 1
    g = np.kron(np.eye(P // GROUP, dtype=f), np.full((GROUP, GROUP), 1.0 / GROUP, f))
    return np.ascontiguousarray(np.concatenate([np.ones((P, 32), f), sel, g], 1))


def kernel(x, L0_conv_gn_w, L0_conv_gn_b, L0_conv_qkv_w, L0_conv_qkv_b, L0_conv_proj_w, L0_conv_proj_b,
           L1_conv_Wq, L1_conv_Wk, L1_conv_Wv, L1_conv_Wout, L1_conv_bout):
    import numpy as np
    import concourse.bacc as bacc
    from concourse.bass_utils import run_bass_kernel_spmd

    def cols(v):
        return np.asarray(v).reshape(-1, P).T

    qkv_w = np.asarray(L0_conv_qkv_w).reshape(8, D, 3, C).transpose(3, 2, 0, 1).reshape(C, 3 * C)
    qkv_b = np.asarray(L0_conv_qkv_b).reshape(8, D, 3).transpose(2, 0, 1).reshape(3 * C)
    wqk = np.concatenate([np.asarray(L1_conv_Wq), np.asarray(L1_conv_Wk)], 1)
    we = np.zeros((P, 2 * C), np.float32)
    we[0:D] = wqk[C:C + D]
    arrays = {
        "x": np.asarray(x).transpose(1, 0, 2, 3).reshape(C, T),
        "params": np.concatenate([cols(L0_conv_gn_w), cols(L0_conv_gn_b), cols(qkv_b[0:2 * C]),
                                  cols(L0_conv_proj_b), cols(L1_conv_bout)], 1),
        "qkv_w": qkv_w,
        "qkv_bv": qkv_b[2 * C:3 * C],
        "proj_w": np.asarray(L0_conv_proj_w).T,
        "w1": wqk[0:C], "w1v": np.asarray(L1_conv_Wv), "w1e": we,
        "wout": np.asarray(L1_conv_Wout),
        "emb": position_embedding(np),
        "consts": constants(np),
    }
    nc = bacc.Bacc("TRN2", target_bir_lowering=False, num_devices=1)
    arrays = {f"in_{k}": np.ascontiguousarray(v) for k, v in arrays.items()}
    ins = {k[3:]: nc.dram_tensor(k, v.shape, F32, kind="ExternalInput").ap() for k, v in arrays.items()}
    out = nc.dram_tensor("out_y", (C, T), F32, kind="ExternalOutput").ap()
    program(nc, **ins, out=out)
    r = run_bass_kernel_spmd(nc, [arrays], core_ids=[0])
    y = np.asarray(r.results[0]["out_y"])
    return np.ascontiguousarray(y.reshape(C, B, 48, 48).transpose(1, 0, 2, 3))
```
